# Optimizing a Trainium2 kernel written in Bass

```python
import numpy as np
import jax
import jax.numpy as jnp

def _softmax(x, axis=-1):
    return jax.nn.softmax(x, axis=axis)

def _gelu(x):
    return jax.nn.gelu(x, approximate=True)

def _silu(x):
    return jax.nn.silu(x)

def _sigmoid(x):
    return jax.nn.sigmoid(x)

def _layernorm(x, axis=-1, eps=1e-05):
    m = jnp.mean(x, axis=axis, keepdims=True)
    v = jnp.var(x, axis=axis, keepdims=True)
    return (x - m) / jnp.sqrt(v + eps)

def _scatter_add(tgt, idx, src, axis=0):
    return tgt.at[idx].add(src)

def _segment_sum(src, seg, n):
    return jax.ops.segment_sum(src, seg, n)
kernel_name = 'mk_adj_resnorm_d1_adj_r2_20b569'

def setup_inputs(seed: int=0):
    np.random.seed(seed)
    _w = jnp.asarray

    def _rec_inputs():
        import jax
        import jax.numpy as jnp
        _gk = jax.random.key(seed)
        x = 0.0002141 + 1 * jax.random.normal(jax.random.fold_in(_gk, 1), (8192, 128), jnp.float32)
        _a = jax.random.bernoulli(jax.random.fold_in(_gk, 2), 0.000976562, (8192, 8192))
        _a = jnp.logical_or(_a, jnp.swapaxes(_a, -1, -2))
        _a = jnp.logical_or(_a, jnp.eye(8192, dtype=bool))
        adj = _a.astype(jnp.int32)
        return (x, adj)
    x, adj = _rec_inputs()

    def _L0_gnn_setup():
        import jax, jax.numpy as jnp
        import numpy as np
        N, IN_DIM, OUT_DIM, K = (3072, 128, 32, 4)
        NEG_SLOPE = 0.2
        key = jax.random.key(seed)
        k1, k2, k3, k4 = jax.random.split(key, 4)
        h = jax.random.normal(k1, (N, IN_DIM), dtype=jnp.float32)
        adj = jax.random.randint(k2, (N, N), 0, 2, dtype=jnp.int32)
        W = jax.random.normal(k3, (OUT_DIM * K, IN_DIM), dtype=jnp.float32) * (1.414 / np.sqrt(IN_DIM))
        a = jax.random.normal(k4, (K, 2 * OUT_DIM), dtype=jnp.float32) * (1.414 / np.sqrt(OUT_DIM))
        return {'h': h, 'adj': adj, 'W': W, 'a': a}
    _L0_gnn_all = _L0_gnn_setup()
    _L0_gnn_in = {k: v for k, v in _L0_gnn_all.items() if k in ('W', 'a')}
    del _L0_gnn_all
    return {'x': x, 'adj': adj, 'L0_gnn_W': _L0_gnn_in['W'], 'L0_gnn_a': _L0_gnn_in['a']}

def reference(x, adj, L0_gnn_W, L0_gnn_a):
    import jax
    import jax.numpy as jnp

    def _L0_gnn_ref(h, adj, W, a):
        import jax, jax.numpy as jnp
        import numpy as np
        N, IN_DIM, OUT_DIM, K = (3072, 128, 32, 4)
        NEG_SLOPE = 0.2
        n = h.shape[0]
        Wh = (h @ W.T).reshape(n, K, OUT_DIM).transpose(1, 0, 2)
        a1 = a[:, :OUT_DIM]
        a2 = a[:, OUT_DIM:]
        score_src = jnp.einsum('knd,kd->kn', Wh, a1)[:, :, None]
        score_dst = jnp.einsum('knd,kd->kn', Wh, a2)[:, None, :]
        e = jax.nn.leaky_relu(score_src + score_dst, NEG_SLOPE)
        e = jnp.where((adj == 0)[None, :, :], -jnp.inf, e)
        alpha = jax.nn.softmax(e, axis=-1)
        alpha = jnp.nan_to_num(alpha, nan=0.0)
        h_prime = jnp.einsum('kij,kjd->kid', alpha, Wh)
        return h_prime.transpose(1, 0, 2).reshape(n, K * OUT_DIM)
    x = _layernorm(x + _L0_gnn_ref(x, adj, L0_gnn_W, L0_gnn_a), axis=-1)
    return x

_drawn_inputs = setup_inputs


def setup_inputs(seed=0):
    import zlib

    import numpy as np

    out = dict(_drawn_inputs(seed))
    spreads = {}
    factors = {}
    for name, (base, spread) in spreads.items():
        noise = np.random.default_rng([zlib.crc32(name.encode()), seed]).standard_normal(out[name].shape)
        drawn = base * np.exp(spread * noise) if base else spread * noise
        out[name] = jnp.asarray(drawn.astype(out[name].dtype))
    for name, factor in factors.items():
        out[name] = (out[name] * factor).astype(out[name].dtype)
    return out
```

```python
from contextlib import ExitStack

import concourse.bass as bass
from concourse import mybir


def gat_layernorm(nc, x, adj, W, a, out):
    fp32, bf16, i32 = mybir.dt.float32, mybir.dt.bfloat16, mybir.dt.int32
    ALU = mybir.AluOpType
    ACT = mybir.ActivationFunctionType
    AX = mybir.AxisListType

    P = 128
    N, D_IN = x.shape
    HEADS, D_OUT = a.shape[0], a.shape[1] // 2
    D_ALL = HEADS * D_OUT
    SLOPE, EPS = 0.2, 1e-5
    STEEP = 2.0 ** 40
    TINY = 1e-37

    IB = 4
    ROWS = IB * P
    GROUPS = N // ROWS
    JB = N // P
    TJ = 4
    TILES = JB // TJ
    OCT = 2 * TJ
    OCTS = JB // OCT
    XT = N // ROWS

    HC = D_OUT + 1
    GH = 2 * HC
    GC = HEADS * GH
    PARTS = 3
    MC = HEADS * HC
    AC = GC + MC
    ACT_HEADS = 2
    PC = D_ALL + 2 * HEADS

    ctx = ExitStack()
    with ctx:
        def sb(name, shape, dt):
            return ctx.enter_context(nc.sbuf_tensor(name, shape, dt))

        def sem(name):
            return ctx.enter_context(nc.semaphore(name))

        G = sb("G", [P, JB, PARTS, GC], bf16)
        s_all = sb("s_all", [P, 2, HEADS, ROWS], fp32)
        adj_t = sb("adj_t", [P, 2, IB, TJ * P], i32)
        conv = sb("conv", [P, 2, IB, TJ * P], bf16)
        mask = sb("mask", [P, 2, ROWS], bf16)
        step = sb("step", [P, 2, ACT_HEADS, ROWS], bf16)
        T = sb("T", [P, 2, HEADS, ROWS], bf16)
        acc_sb = sb("acc_sb", [P, IB, AC], fp32)
        xr = sb("xr", [P, 2, IB, D_IN], fp32)
        xT = sb("xT", [P, 2, ROWS], fp32)
        y = sb("y", [P, 2, IB, D_IN], fp32)
        proj = sb("proj", [P, PC], fp32)
        w_sb = sb("w_sb", [P, D_IN], fp32)
        a_blk = sb("a_blk", [P, 2 * HEADS], fp32)
        identf = sb("identf", [P, P], fp32)
        identb = sb("identb", [P, P], bf16)
        zeros = sb("zeros", [P, P], bf16)
        s_row = sb("s_row", [HEADS, 2, ROWS], fp32)
        sd = sb("sd", [P, JB, 2 * HEADS], fp32)
        d_neg = sb("d_neg", [P, JB, HEADS], fp32)
        d_steep = sb("d_steep", [P, JB, HEADS], fp32)
        Bv = sb("Bv", [P, JB, HEADS], fp32)
        Fv = sb("Fv", [P, JB, HEADS], fp32)
        alpha = sb("alpha", [P, JB, HEADS], fp32)
        beta = sb("beta", [P, JB, HEADS], fp32)
        d_part = sb("d_part", [P, HEADS], fp32)
        d_max = sb("d_max", [P, HEADS], fp32)
        wide = sb("wide", [P, 2, TJ, GC], fp32)
        rden = sb("rden", [P, IB, HEADS], fp32)
        stats = sb("stats", [P, IB, 6], fp32)
        mv = sb("mv", [P, IB, 2], fp32)
        rstd = sb("rstd", [P, IB], fp32)
        eps_t = sb("eps_t", [P, 1], fp32)
        half_t = sb("half_t", [P, IB], fp32)
        Wh = G[:, :, :, :].rearrange("p j s c -> p j (s c)").bitcast(fp32)[:, :, 0:D_ALL]

        bank = [ctx.enter_context(nc.psum_tensor(f"bank{n}", [P, 512], fp32)) for n in range(8)]
        acc, tr, sp = bank[0:4], bank[4:6], bank[6:8]
        trb = [t[:, :].bitcast(bf16) for t in tr]

        sT = nc.dram_tensor("sT_scratch", [HEADS, N], fp32, kind="Internal").ap()

        x_v = x.rearrange("(t b p) f -> t p b f", b=IB, p=P)
        o_v = out.rearrange("(t b p) f -> t p b f", b=IB, p=P)
        adj_v = adj.rearrange("(g b p) (c n) -> g c p b n", b=IB, p=P, n=TJ * P)
        sT_v = sT.rearrange("h (t n) -> t h n", n=ROWS)

        consts_set = sem("consts_set")
        w_loaded = sem("w_loaded")
        x_loaded = [sem(f"x_loaded{n}") for n in range(2)]
        xT_psum = sem("xT_psum")
        xT_copied = sem("xT_copied")
        wT_psum = sem("wT_psum")
        proj_set = sem("proj_set")
        wh_psum = sem("wh_psum")
        wh_copied = sem("wh_copied")
        s_copied = sem("s_copied")
        s_stored = sem("s_stored")
        s_loaded = [sem(f"s_loaded{n}") for n in range(2)]
        d_part_set = sem("d_part_set")
        d_max_set = sem("d_max_set")
        args_set = sem("args_set")
        exps_set = sem("exps_set")
        wide_set = sem("wide_set")
        part_set = sem("part_set")
        rest1_set = sem("rest1_set")
        rest2_set = sem("rest2_set")
        adj_loaded = [sem(f"adj_loaded{n}") for n in range(2)]
        converted = sem("converted")
        begun = sem("begun")
        transposed = sem("transposed")
        mask_set = sem("mask_set")
        step_set = sem("step_set")
        T_dve = sem("T_dve")
        T_act = sem("T_act")
        block_done = sem("block_done")
        acc_done = sem("acc_done")
        acc_dve = sem("acc_dve")
        acc_act = sem("acc_act")
        res_loaded = [sem(f"res_loaded{n}") for n in range(2)]
        var_set = sem("var_set")
        rstd_set = sem("rstd_set")
        y_set = sem("y_set")
        stored = sem("stored")
        dve_chain = sem("dve_chain")

        block = ctx.enter_context(nc.Block())

        LEAD = 2

        def done(n):
            return n + LEAD

        def freed(n):
            return done(n - 1)

        @block.sync
        def _(sync):
            sync.sem_inc(stored, 16 * LEAD)
            sync.sem_inc(s_stored, 16 * LEAD)
            sync.dma_start(w_sb[:, :], W[:, :]).then_inc(w_loaded, 16)
            sync.wait_ge(consts_set, 1)
            for h in range(HEADS):
                for side in range(2):
                    sync.dma_start(a_blk[h * D_OUT:(h + 1) * D_OUT, side * HEADS + h:side * HEADS + h + 1],
                                   a[h:h + 1, side * D_OUT:(side + 1) * D_OUT].rearrange("o n -> n o")
                                   ).then_inc(w_loaded, 16)

            def x_tile(t, n, waits):
                if waits:
                    sync.wait_ge(xT_psum, t - 1)
                sync.dma_start(xr[:, n], x_v[t]).then_inc(x_loaded[n], 16)

            def s_store(t, n):
                sync.wait_ge(s_copied, done(t + 1))
                sync.dma_start(sT_v[t], s_row[:, n]).then_inc(s_stored, 16)

            x_tile(0, 0, False)
            x_tile(1, 1, False)

            def adj_tile(g, c, t, n):
                sync.wait_ge(converted, freed(t))
                sync.dma_start(adj_t[:, n], adj_v[g, c]).then_inc(adj_loaded[n], 16)

            with sync.Fori(0, XT // 2 - 1) as u:
                t = 2 * u
                for n in range(2):
                    x_tile(t + n + 2, n, True)
                    s_store(t + n, n)
            for n in range(2):
                s_store(XT - 2 + n, n)
            sync.wait_ge(s_stored, 16 * done(XT))

            def load_s(g, n):
                src = sT_v[g].unsqueeze(0).to_broadcast([P, HEADS, ROWS])
                sync.dma_start(s_all[:, n], src).then_inc(s_loaded[n], 16)

            load_s(0, 0)

            def tiles(g, lo, hi):
                with sync.Fori(lo // 2, hi // 2) as u:
                    c = 2 * u
                    for n in range(2):
                        adj_tile(g, c + n, g * TILES + c + n, n)

            def group(g, n, first=False, last=False):
                tiles(g, 0, TILES // 2)
                if not first:
                    sync.wait_ge(y_set, done(g))
                    sync.dma_start(o_v[g - 1], y[:, 1 - n]).then_inc(stored, 16)
                if not last:
                    load_s(g + 1, 1 - n)
                sync.dma_start(xr[:, n], x_v[g]).then_inc(res_loaded[n], 16)
                tiles(g, TILES // 2, TILES)

            group(0, 0, first=True)
            with sync.Fori(0, GROUPS // 2 - 1) as u:
                g = 2 * u + 1
                group(g, 1)
                group(g + 1, 0)
            group(GROUPS - 1, 1, last=True)
            sync.wait_ge(y_set, done(GROUPS))
            sync.dma_start(o_v[GROUPS - 1], y[:, 1]).then_inc(stored, 16)
            sync.wait_ge(stored, 16 * done(GROUPS))

        @block.gpsimd
        def _(pool):
            pool.sem_inc(converted, LEAD)
            nc.gpsimd.memset(a_blk[:, :], 0.0)
            nc.gpsimd.memset(zeros[:, :], 0.0)
            nc.gpsimd.memset(eps_t[:, :], EPS)
            nc.gpsimd.memset(half_t[:, :], -0.5)
            nc.gpsimd.memset(identb[:, :], 0.0)
            nc.gpsimd.memset(identf[:, :], 0.0).then_inc(consts_set, 1)
            pool.wait_ge(consts_set, 1)
            nc.gpsimd.affine_select(out=identb[:, :], in_=identb[:, :], compare_op=ALU.not_equal, fill=1.0,
                                    base=0, pattern=[[-1, P]], channel_multiplier=1).then_inc(consts_set, 1)
            nc.gpsimd.affine_select(out=identf[:, :], in_=identf[:, :], compare_op=ALU.not_equal, fill=1.0,
                                    base=0, pattern=[[-1, P]], channel_multiplier=1).then_inc(consts_set, 1)

            pool.wait_ge(d_part_set, 1)
            nc.gpsimd.partition_all_reduce(d_max[:, :], d_part[:, :], P, bass.bass_isa.ReduceOp.max).then_inc(d_max_set, 1)

            with pool.Fori(0, JB // TJ // 2) as u:
                m = 2 * u
                for n in range(2):
                    pool.wait_ge(part_set, done(3 * m + n + 3))
                    nc.gpsimd.tensor_tensor(wide[:, n], wide[:, n], G[:, bass.ds((m + n) * TJ, TJ), 1, :],
                                            ALU.subtract).then_inc(rest2_set, 1)

            def convert(t, n, pair):
                pool.wait_ge(adj_loaded[n], 16 * pair + 16)
                pool.wait_ge(transposed, (t + 1) * TJ)
                pool.sem_inc(begun, 1)
                nc.gpsimd.tensor_scalar(conv[:, n], adj_t[:, n], 1.0, -1.0, ALU.min, ALU.max).then_inc(converted, 1)

            def pairs(g, lo, hi):
                with pool.Fori(lo, hi) as c:
                    for n in range(2):
                        pair = g * (TILES // 2) + c
                        convert(2 * pair + n, n, pair)

            def inverse_deviation(g):
                pool.wait_ge(var_set, g + 1)
                nc.gpsimd.tensor_tensor(rstd[:, :], mv[:, :, 1], half_t[:, :], ALU.pow).then_inc(rstd_set, 1)

            pairs(0, 0, TILES // 2)
            with pool.Fori(1, GROUPS) as g:
                pairs(g, 0, 2)
                inverse_deviation(g - 1)
                pairs(g, 2, TILES // 2)
            inverse_deviation(GROUPS - 1)

        @block.scalar
        def _(act):
            for ready in (mask_set, part_set, xT_copied, s_copied, acc_act):
                act.sem_inc(ready, LEAD)
            act.wait_ge(wT_psum, 1)
            nc.scalar.copy(proj[:, :], sp[0][:, 0:PC]).then_inc(proj_set, 1)
            with act.Fori(0, XT // 2) as u:
                t = 2 * u
                for n in range(2):
                    act.wait_ge(xT_psum, t + n + 1)
                    if n == 0:
                        act.wait_ge(wh_psum, done(t))
                    nc.scalar.copy(xT[:, n], tr[n][:, :]).then_inc(xT_copied, 1)
                for n in range(2):
                    act.wait_ge(wh_psum, done(t + n + 1))
                    act.wait_ge(s_stored, 16 * done(t))
                    nc.scalar.copy(s_row[:, n], sp[n][0:HEADS, :]).then_inc(s_copied, 1)

            act.wait_ge(args_set, 1)
            nc.scalar.activation(Bv[:, :, :], Bv[:, :, :], ACT.Exp)
            nc.scalar.activation(Fv[:, :, :], Fv[:, :, :], ACT.Exp, scale=SLOPE)
            nc.scalar.activation(alpha[:, :, :], alpha[:, :, :], ACT.Exp)
            nc.scalar.activation(beta[:, :, :], beta[:, :, :], ACT.Exp).then_inc(exps_set, 1)

            with act.Fori(0, JB // TJ // 2) as u:
                m = 2 * u
                for part, ready in ((0, wide_set), (1, rest1_set), (2, rest2_set)):
                    for n in range(2):
                        act.wait_ge(ready, m + n + 1)
                        nc.scalar.copy(G[:, bass.ds((m + n) * TJ, TJ), part, :], wide[:, n]).then_inc(part_set, 1)

            def blocks(g, n, q, j, only):
                for k in only:
                    b = k % 2
                    act.wait_ge(transposed, q + k + 1 + 2 * TJ)
                    act.wait_ge(block_done, freed(q + k))
                    nc.scalar.activation(mask[:, b], trb[b][:, 0:ROWS], ACT.Square).then_inc(mask_set, 1)
                    act.wait_ge(T_act, freed(q + k))
                    for h in range(ACT_HEADS):
                        nc.scalar.activation(step[:, b, h], s_all[:, n, h], ACT.Sigmoid, scale=STEEP,
                                             bias=d_steep[:, bass.ds(j + k, 1), h]).then_inc(step_set, 1)

            def take_sums(g):
                act.wait_ge(acc_done, g + 1)
                act.wait_ge(y_set, done(g))
                for b in (2, 3):
                    nc.scalar.copy(acc_sb[:, b], acc[b][:, 0:AC]).then_inc(acc_act, 1)

            def group(g, n, first=False):
                act.wait_ge(s_loaded[n], 8 * (g + 2 - n))
                blocks(g, n, g * JB, 0, [0])
                if not first:
                    take_sums(g - 1)
                blocks(g, n, g * JB, 0, range(1, OCT))
                with act.Fori(1, OCTS) as o:
                    blocks(g, n, g * JB + o * OCT, o * OCT, range(OCT))

            group(0, 0, first=True)
            with act.Fori(0, GROUPS // 2 - 1) as u:
                g = 2 * u + 1
                group(g, 1)
                group(g + 1, 0)
            group(GROUPS - 1, 1)
            take_sums(GROUPS - 1)

        @block.vector
        def _(dve):
            links = [0]

            def link(ins):
                links[0] += 1
                ins.then_inc(dve_chain, 1)
                return links[0]

            for ready in (T_act, T_dve, wh_copied, acc_dve, y_set):
                dve.sem_inc(ready, LEAD)

            with dve.Fori(0, XT // 2) as u:
                t = 2 * u
                for n in range(2):
                    dve.wait_ge(wh_psum, done(t + n + 1))
                    for half in range(2):
                        src = acc[2 * n + half][:, 0:2 * PC].rearrange("p (b c) -> p b c", b=2)
                        blk = bass.ds((t + n) * IB + 2 * half, 2)
                        nc.vector.tensor_copy(Wh[:, blk, :], src[:, :, 0:D_ALL])
                        nc.vector.tensor_copy(sd[:, blk, :], src[:, :, D_ALL:PC]).then_inc(wh_copied, 1)
            dve.wait_ge(wh_copied, done(2 * XT))
            s_c, d_c = sd[:, :, 0:HEADS], sd[:, :, HEADS:2 * HEADS]
            nc.vector.tensor_reduce(d_part[:, :], d_c.rearrange("p j h -> p h j"), AX.X, ALU.max).then_inc(d_part_set, 1)
            nc.vector.tensor_scalar(d_neg[:, :, :], d_c, -1.0, None, ALU.mult)
            nc.vector.tensor_scalar(d_steep[:, :, :], d_c, STEEP, None, ALU.mult)
            dve.wait_ge(d_max_set, 1)
            D_b = d_max[:, :].unsqueeze(1).to_broadcast([P, JB, HEADS])
            nc.vector.tensor_tensor(Bv[:, :, :], d_c, D_b, ALU.subtract)
            nc.vector.tensor_tensor(Fv[:, :, :], d_c, D_b, ALU.subtract)
            dve.wait_ge(dve_chain, link(nc.vector.tensor_tensor(alpha[:, :, :], s_c, D_b, ALU.add)))
            dve.wait_ge(dve_chain, link(nc.vector.scalar_tensor_tensor(
                beta[:, :, :], alpha[:, :, :], SLOPE, alpha[:, :, :], ALU.mult, ALU.max)))
            zs = wide[:, 0].rearrange("p t c -> p (t c)")[:, 0:JB * HEADS].rearrange("p (j h) -> p j h", h=HEADS)
            dve.wait_ge(dve_chain, link(nc.vector.tensor_tensor(zs, alpha[:, :, :], beta[:, :, :], ALU.subtract)))
            dve.wait_ge(dve_chain, link(nc.vector.scalar_tensor_tensor(
                beta[:, :, :], alpha[:, :, :], SLOPE, beta[:, :, :], ALU.mult, ALU.subtract)))
            nc.vector.tensor_copy(alpha[:, :, :], zs).then_inc(args_set, 1)
            dve.wait_ge(exps_set, 1)

            def weigh(m, n):
                blk = bass.ds((m + n) * TJ, TJ)
                wh = Wh[:, blk, :].rearrange("p j (h c) -> p j h c", h=HEADS)
                dst = wide[:, n].rearrange("p j (h c) -> p j h c", h=HEADS)
                for k, v in enumerate((Bv, Fv)):
                    vb = v[:, blk, :]
                    nc.vector.tensor_copy(dst[:, :, :, k * HC + D_OUT], vb)
                    last = nc.vector.tensor_tensor(dst[:, :, :, k * HC:k * HC + D_OUT], wh,
                                                   vb.unsqueeze(3).to_broadcast([P, TJ, HEADS, D_OUT]), ALU.mult)
                last.then_inc(wide_set, 1)

            dve.wait_ge(args_set, 1)
            with dve.Fori(0, JB // TJ // 2) as u:
                m = 2 * u
                dve.wait_ge(part_set, done(3 * m))
                for n in range(2):
                    weigh(m, n)
                for n in range(2):
                    dve.wait_ge(part_set, done(3 * m + n + 1))
                    nc.vector.tensor_tensor(wide[:, n], wide[:, n], G[:, bass.ds((m + n) * TJ, TJ), 0, :],
                                            ALU.subtract).then_inc(rest1_set, 1)

            def blocks(g, n, q, j, only):
                for k in only:
                    b = k % 2
                    dve.wait_ge(mask_set, done(q + k + 1))
                    dve.wait_ge(block_done, freed(q + k))
                    for h in range(ACT_HEADS, HEADS):
                        last = nc.vector.scalar_tensor_tensor(T[:, b, h], s_all[:, n, h], d_neg[:, bass.ds(j + k, 1), h],
                                                              mask[:, b], ALU.is_ge, ALU.mult)
                    last.then_inc(T_dve, 1)
                    dve.wait_ge(step_set, ACT_HEADS * (q + k + 1))
                    nc.vector.tensor_tensor(T[:, b, 0:ACT_HEADS], step[:, b],
                                            mask[:, b].unsqueeze(1).to_broadcast([P, ACT_HEADS, ROWS]),
                                            ALU.mult).then_inc(T_act, 1)
                    yield

            def finish(g, n):
                got = [0]

                def wait_last(ins):
                    got[0] += 1
                    ins.then_inc(dve_chain, 1)
                    dve.wait_ge(dve_chain, CHAIN0 + g * CHAIN_STEP + got[0])

                t_part = acc_sb[:, :, 0:GC].rearrange("p b (h c) -> p b h c", h=HEADS)
                m_part = acc_sb[:, :, GC:AC].rearrange("p b (h c) -> p b h c", h=HEADS)
                rows = bass.ds(g * IB, IB)

                def per_row(v):
                    return v[:, rows, :].unsqueeze(3).to_broadcast([P, IB, HEADS, HC])

                top, low = t_part[:, :, :, 0:HC], t_part[:, :, :, HC:GH]
                dve.wait_ge(acc_act, done(2 * g + 2))
                dve.wait_ge(acc_dve, done(2 * g + 2))
                wait_last(nc.vector.tensor_tensor(m_part, m_part, low, ALU.subtract))
                yield
                nc.vector.tensor_tensor(top, top, per_row(alpha), ALU.mult)
                wait_last(nc.vector.tensor_tensor(m_part, m_part, per_row(beta), ALU.mult))
                yield
                wait_last(nc.vector.tensor_tensor(top, top, m_part, ALU.add))
                yield
                wait_last(nc.vector.tensor_scalar(rden[:, :, :], top[:, :, :, D_OUT], TINY, None, ALU.max))
                wait_last(nc.vector.reciprocal(rden[:, :, :], rden[:, :, :]))
                yv = y[:, n].rearrange("p b (h c) -> p b h c", h=HEADS)
                dve.wait_ge(stored, 16 * (g + 1))
                wait_last(nc.vector.tensor_tensor(yv, top[:, :, :, 0:D_OUT],
                                                  rden[:, :, :].unsqueeze(3).to_broadcast([P, IB, HEADS, D_OUT]), ALU.mult))
                yield
                dve.wait_ge(res_loaded[n], 8 * (g + 2 - n))
                wait_last(nc.vector.tensor_tensor(y[:, n], y[:, n], xr[:, n], ALU.add))
                yield
                for b in range(IB):
                    last = nc.vector.bn_stats(stats[:, b], y[:, n, b])
                wait_last(last)
                yield
                for b in range(IB):
                    last = nc.vector.bn_aggr(mv[:, b], stats[:, b])
                wait_last(last)
                nc.vector.tensor_scalar(mv[:, :, 1], mv[:, :, 1], EPS, None, ALU.add).then_inc(var_set, 1)
                yield
                yield
                dve.wait_ge(rstd_set, g + 1)
                for b in range(IB):
                    last = nc.vector.tensor_scalar(y[:, n, b], y[:, n, b], mv[:, b, 0:1], rstd[:, b:b + 1],
                                                   ALU.subtract, ALU.mult)
                last.then_inc(y_set, 1)

            CHAIN0, CHAIN_STEP = links[0], 9

            def take_sums(g):
                dve.wait_ge(acc_done, g + 1)
                for b in (0, 1):
                    nc.vector.tensor_copy(acc_sb[:, b], acc[b][:, 0:AC]).then_inc(acc_dve, 1)

            def group(g, n, first=False):
                dve.wait_ge(s_loaded[n], 8 * (g + 2 - n))
                steps = blocks(g, n, g * JB, 0, range(OCT))
                next(steps)
                if first:
                    for _ in steps:
                        pass
                else:
                    take_sums(g - 1)
                    closing = finish(g - 1, 1 - n)
                    for _ in steps:
                        next(closing, None)
                    steps = blocks(g, n, g * JB + OCT, OCT, range(OCT))
                    for _ in steps:
                        next(closing, None)
                    for _ in closing:
                        pass
                with dve.Fori(1 if first else 2, OCTS) as o:
                    for _ in blocks(g, n, g * JB + o * OCT, o * OCT, range(OCT)):
                        pass

            group(0, 0, first=True)
            with dve.Fori(0, GROUPS // 2 - 1) as u:
                g = 2 * u + 1
                group(g, 1)
                group(g + 1, 0)
            group(GROUPS - 1, 1)
            take_sums(GROUPS - 1)
            for _ in finish(GROUPS - 1, 1):
                pass

        @block.tensor
        def _(pe):
            pe.sem_inc(transposed, 2 * TJ)
            pe.sem_inc(block_done, LEAD)
            pe.sem_inc(wh_psum, LEAD)
            pe.wait_ge(consts_set, 3)
            pe.wait_ge(w_loaded, 16 * (1 + 2 * HEADS))
            nc.tensor.transpose(sp[0][:, 0:P], w_sb[:, :], identf[:, :])
            nc.tensor.matmul(sp[0][:, P:PC], w_sb[:, :], a_blk[:, :], start=True, stop=True).then_inc(wT_psum, 1)
            pe.wait_ge(proj_set, 1)

            with pe.Fori(0, XT // 2) as u:
                t = 2 * u
                for n in range(2):
                    pe.wait_ge(x_loaded[n], 8 * t + 16)
                    pe.wait_ge(xT_copied, done(t))
                    for b in range(IB):
                        last = nc.tensor.transpose(tr[n][:, b * P:(b + 1) * P], xr[:, n, b], identf[:, :])
                    last.then_inc(xT_psum, 1)
                for n in range(2):
                    pe.wait_ge(xT_copied, done(t + n + 1))
                    if n == 0:
                        pe.wait_ge(wh_copied, done(2 * t))
                        pe.wait_ge(s_copied, done(t))
                    for b in range(IB):
                        nc.tensor.matmul(acc[2 * n + b // 2][:, (b % 2) * PC:(b % 2 + 1) * PC],
                                         xT[:, n, b * P:(b + 1) * P], proj[:, :], start=True, stop=True)
                    nc.tensor.matmul(sp[n][0:HEADS, :], proj[:, D_ALL:D_ALL + HEADS], xT[:, n],
                                     start=True, stop=True).then_inc(wh_psum, 1)

            def transpose_block(q, tile, k):
                b = k % 2
                if k % TJ == 0:
                    pe.wait_ge(converted, done(tile + k // TJ + 1))
                pe.wait_ge(mask_set, freed(q + k))
                for r in range(IB):
                    last = nc.tensor.transpose(trb[b][:, r * P:(r + 1) * P],
                                               conv[:, (k // TJ) % 2, r, (k % TJ) * P:(k % TJ + 1) * P], identb[:, :])
                last.then_inc(transposed, 1)

            def add_block(q, j, k):
                b = k % 2

                def add(lhsT, part, cols, dst):
                    return nc.tensor.matmul(dst, lhsT, cols[:, j + k, part], start=False, stop=False,
                                            skip_group_check=True)

                pe.wait_ge(mask_set, done(q + k + 1))
                low = G[:, :, :, :].rearrange("p j s (h c) -> p j s h c", h=HEADS)[:, :, :, :, HC:GH]
                for r in range(IB):
                    dst = acc[r][:, GC:AC].rearrange("p (h c) -> p h c", h=HEADS)
                    for part in range(PARTS):
                        add(mask[:, b, r * P:(r + 1) * P], part, low, dst)
                for heads, ready in ((range(ACT_HEADS, HEADS), T_dve), (range(ACT_HEADS), T_act)):
                    pe.wait_ge(ready, done(q + k + 1))
                    for h in heads:
                        for r in range(IB):
                            for part in range(PARTS):
                                last = add(T[:, b, h, r * P:(r + 1) * P], part, G[:, :, :, h * GH:(h + 1) * GH],
                                           acc[r][:, h * GH:(h + 1) * GH])
                last.then_inc(block_done, 1)

            def octet(g, o, ahead):
                q, tile, j = g * JB + o * OCT, g * TILES + o * (OCT // TJ), o * OCT
                for k in range(OCT):
                    if k + 2 < OCT or ahead:
                        transpose_block(q, tile, k + 2)
                    add_block(q, j, k)

            def open_sums(g):
                pe.wait_ge(acc_dve, done(2 * g))
                pe.wait_ge(acc_act, done(2 * g))
                for r in range(IB):
                    nc.tensor.matmul(acc[r][:, AC:AC + 2], zeros[:, :], zeros[:, 0:2], start=True, stop=False,
                                     skip_group_check=True)

            def close_sums():
                for r in range(IB):
                    last = nc.tensor.matmul(acc[r][:, AC:AC + 2], zeros[:, :], zeros[:, 0:2], start=False, stop=True,
                                            skip_group_check=True)
                last.then_inc(acc_done, 1)

            pe.wait_ge(part_set, done(3 * (JB // TJ)))
            pe.wait_ge(s_copied, done(XT))
            for k in range(2):
                transpose_block(0, 0, k)
            with pe.Fori(0, GROUPS - 1) as g:
                open_sums(g)
                with pe.Fori(0, OCTS) as o:
                    octet(g, o, True)
                close_sums()
            open_sums(GROUPS - 1)
            with pe.Fori(0, OCTS - 1) as o:
                octet(GROUPS - 1, o, True)
            octet(GROUPS - 1, OCTS - 1, False)
            close_sums()


_INS = ["x", "adj", "L0_gnn_W", "L0_gnn_a"]


def kernel(**inputs):
    import numpy as np
    import concourse.bacc as bacc
    from concourse.bass_utils import run_bass_kernel_spmd

    nc = bacc.Bacc("TRN2", target_bir_lowering=False, num_devices=1)
    arrays, args = {}, []
    for name in _INS:
        v = np.ascontiguousarray(inputs[name])
        arrays[f"in_{name}"] = v
        args.append(nc.dram_tensor(f"in_{name}", v.shape, mybir.dt.from_np(v.dtype), kind="ExternalInput").ap())
    shape = inputs["x"].shape
    args.append(nc.dram_tensor("out", shape, mybir.dt.float32, kind="ExternalOutput").ap())
    gat_layernorm(nc, *args)
    r = run_bass_kernel_spmd(nc, [arrays], core_ids=[0])
    return r.results[0]["out"]
```

```python
from contextlib import ExitStack

import concourse.bass as bass
from concourse import mybir


def gat_layernorm(nc, x, adj, W, a, out):
    fp32, bf16, fp16, i32 = mybir.dt.float32, mybir.dt.bfloat16, mybir.dt.float16, mybir.dt.int32
    ALU = mybir.AluOpType
    ACT = mybir.ActivationFunctionType
    AX = mybir.AxisListType

    P = 128
    N, D_IN = x.shape
    HEADS, D_OUT = a.shape[0], a.shape[1] // 2
    D_ALL = HEADS * D_OUT
    SLOPE, EPS = 0.2, 1e-5
    STEEP = 2.0 ** 40
    EXPONENT_BITS = 0x7F800000
    TINY = 1e-37

    IB = 4
    ROWS = IB * P
    GROUPS = N // ROWS
    JB = N // P
    TJ = 4
    TILES = JB // TJ
    OCT = 2 * TJ
    OCTS = JB // OCT
    XT = N // ROWS

    NM = 4
    HC = D_OUT + 1
    BP, FP = 3, 2
    BC, FC = BP * HC, FP * HC
    CH = BC + FC
    CHUNKS = IB * HEADS
    PER_BANK = 512 // CH
    BANKS = -(-CHUNKS // PER_BANK)
    USED = PER_BANK * CH
    ACT_HEADS = 3
    PC = D_ALL + 2 * HEADS

    ctx = ExitStack()
    with ctx:
        def sb(name, shape, dt):
            return ctx.enter_context(nc.sbuf_tensor(name, shape, dt))

        def sem(name):
            return ctx.enter_context(nc.semaphore(name))

        G_words = sb("G", [P, JB, HEADS * BC], bf16)
        G = G_words[:, :, :].rearrange("p j (h s c) -> p j h s c", h=HEADS, s=BP)
        F = sb("F", [P, JB, HEADS, FP, HC], fp16)
        M = sb("M", [P, JB, HEADS, FP, HC], fp16)
        s_all = sb("s_all", [P, 2, HEADS, ROWS], fp32)
        adj_t = sb("adj_t", [P, 2, IB, TJ * P], i32)
        conv = sb("conv", [P, 2, IB, TJ * P], bf16)
        mask = sb("mask", [P, NM, ROWS], bf16)
        step = sb("step", [P, 2, ACT_HEADS, ROWS], bf16)
        T = sb("T", [P, 2, HEADS, ROWS], bf16)
        xr = sb("xr", [P, 2, IB, D_IN], fp32)
        res, y = xr[:, 0], xr[:, 1]
        T_words = T[:, :, :, :].rearrange("p n h r -> p (n h r)").bitcast(fp32)
        w_sb, identf, proj = T_words[:, 0:D_IN], T_words[:, D_IN:D_IN + P], T_words[:, D_IN + P:D_IN + P + PC]
        a_blk = sb("a_blk", [P, 2 * HEADS], fp32)
        identb = sb("identb", [P, P], bf16)
        zeros = sb("zeros", [P, 2], bf16)
        d_act = sb("d_act", [P, OCT, ACT_HEADS], fp32)
        d_dve = sb("d_dve", [P, OCT, HEADS - ACT_HEADS], fp32)
        s_row = step[0:HEADS].rearrange("p n h r -> p (n h r)").bitcast(fp32)[:, 0:2 * ROWS].rearrange("p (n r) -> p n r", n=2)
        sd = sb("sd", [P, JB, 2 * HEADS], fp32)
        d_steep, d_neg = sd[:, :, 0:HEADS], sd[:, :, HEADS:2 * HEADS]
        Bv, Fv = (s_all[:, 1, h, 0:JB * HEADS].rearrange("p (j h) -> p j h", h=HEADS) for h in range(2))
        alpha = sb("alpha", [P, JB, HEADS], fp32)
        beta = sb("beta", [P, JB, HEADS], fp32)
        d_part = sb("d_part", [P, HEADS], fp32)
        d_max = sb("d_max", [P, HEADS], fp32)
        wh_part = sb("wh_part", [P, 2 * XT], fp32)
        wh_big = sb("wh_big", [P, 2], fp32)
        sigma = sb("sigma", [P, 2], fp32)
        late = sb("late", [P, CHUNKS * CH], fp32)
        wide = late[:, 0:2 * TJ * HEADS * 2 * HC].rearrange("p (n t h k c) -> p n t h k c", n=2, t=TJ, h=HEADS, k=2)
        xT = late[:, 0:2 * ROWS].rearrange("p (n r) -> p n r", n=2)
        acc_sb = late[:, :].rearrange("p (k c) -> p k c", c=CH)
        rden = sb("rden", [P, IB, HEADS], fp32)
        stats = sb("stats", [P, IB, 6], fp32)
        mv = sb("mv", [P, IB, 2], fp32)
        rstd = sb("rstd", [P, IB], fp32)
        eps_t = sb("eps_t", [P, 1], fp32)
        half_t = sb("half_t", [P, IB], fp32)
        Wh = G_words[:, :, :].bitcast(fp32)[:, :, 0:D_ALL]

        bank = [ctx.enter_context(nc.psum_tensor(f"bank{n}", [P, 512], fp32)) for n in range(8)]
        acc, tr, sp = bank[0:BANKS], bank[BANKS:8], bank[BANKS - 2:BANKS]
        trb = [t[:, :].bitcast(bf16) for t in tr]

        sT = nc.dram_tensor("sT_scratch", [HEADS, N], fp32, kind="Internal").ap()

        x_v = x.rearrange("(t b p) f -> t p b f", b=IB, p=P)
        o_v = out.rearrange("(t b p) f -> t p b f", b=IB, p=P)
        adj_v = adj.rearrange("(g b p) (c n) -> g c p b n", b=IB, p=P, n=TJ * P)
        sT_v = sT.rearrange("h (t n) -> t h n", n=ROWS)

        consts_set = sem("consts_set")
        w_loaded = sem("w_loaded")
        x_loaded = [sem(f"x_loaded{n}") for n in range(2)]
        xT_psum = sem("xT_psum")
        xT_copied = sem("xT_copied")
        wT_psum = sem("wT_psum")
        proj_set = sem("proj_set")
        wh_psum = sem("wh_psum")
        wh_copied = sem("wh_copied")
        s_copied = sem("s_copied")
        s_stored = sem("s_stored")
        s_loaded = [sem(f"s_loaded{n}") for n in range(2)]
        d_part_set = sem("d_part_set")
        d_max_set = sem("d_max_set")
        args_set = sem("args_set")
        exps_set = sem("exps_set")
        wide_set = sem("wide_set")
        part_set = sem("part_set")
        f_set = sem("f_set")
        m_set = sem("m_set")
        rest1_set = sem("rest1_set")
        rest2_set = sem("rest2_set")
        adj_loaded = [sem(f"adj_loaded{n}") for n in range(2)]
        converted = sem("converted")
        begun = sem("begun")
        transposed = sem("transposed")
        mask_set = sem("mask_set")
        step_set = sem("step_set")
        d_act_set = sem("d_act_set")
        d_dve_set = sem("d_dve_set")
        T_dve = sem("T_dve")
        T_act = sem("T_act")
        early_done = sem("early_done")
        block_done = sem("block_done")
        acc_done = sem("acc_done")
        acc_dve = sem("acc_dve")
        acc_act = sem("acc_act")
        res_loaded = sem("res_loaded")
        var_set = sem("var_set")
        rstd_set = sem("rstd_set")
        y_set = sem("y_set")
        stored = sem("stored")
        dve_chain = sem("dve_chain")

        def chunks_of(b):
            return min(PER_BANK, CHUNKS - b * PER_BANK)

        def counts(eng, q, n):
            return [q + k + 1 if isinstance(q, int) else eng.snap(q + k + 1) for k in range(n)]

        block = ctx.enter_context(nc.Block())

        LEAD = 2

        def done(n):
            return n + LEAD

        def freed(n):
            return done(n - 1)

        @block.sync
        def _(sync):
            sync.sem_inc(stored, 16 * LEAD)
            sync.sem_inc(s_stored, 16 * LEAD)
            sync.dma_start(w_sb, W[:, :]).then_inc(w_loaded, 16)
            sync.wait_ge(consts_set, 1)
            for h in range(HEADS):
                for side in range(2):
                    sync.dma_start(a_blk[h * D_OUT:(h + 1) * D_OUT, side * HEADS + h:side * HEADS + h + 1],
                                   a[h:h + 1, side * D_OUT:(side + 1) * D_OUT].rearrange("o n -> n o")
                                   ).then_inc(w_loaded, 16)

            def x_tile(t, n, waits):
                if waits:
                    sync.wait_ge(xT_psum, t - 1)
                sync.dma_start(xr[:, n], x_v[t]).then_inc(x_loaded[n], 16)

            def s_store(t, n):
                sync.wait_ge(s_copied, done(t + 1))
                sync.dma_start(sT_v[t], s_row[:, n]).then_inc(s_stored, 16)

            x_tile(0, 0, False)
            x_tile(1, 1, False)

            def adj_tile(g, c, t, n):
                sync.wait_ge(converted, freed(t))
                sync.dma_start(adj_t[:, n], adj_v[g, c]).then_inc(adj_loaded[n], 16)

            with sync.Fori(0, XT // 2 - 1) as u:
                t = 2 * u
                for n in range(2):
                    x_tile(t + n + 2, n, True)
                    s_store(t + n, n)
            for n in range(2):
                s_store(XT - 2 + n, n)
            sync.wait_ge(s_stored, 16 * done(XT))

            def load_s(g, n):
                src = sT_v[g].unsqueeze(0).to_broadcast([P, HEADS, ROWS])
                sync.dma_start(s_all[:, n], src).then_inc(s_loaded[n], 16)

            load_s(0, 0)

            def tiles(g, lo, hi):
                with sync.Fori(lo // 2, hi // 2) as u:
                    c = 2 * u
                    for n in range(2):
                        adj_tile(g, c + n, g * TILES + c + n, n)

            def group(g, n, first=False, last=False):
                tiles(g, 0, TILES // 2)
                if not first:
                    sync.wait_ge(y_set, done(g))
                    sync.dma_start(o_v[g - 1], y).then_inc(stored, 16)
                else:
                    sync.wait_ge(part_set, done(3 * (JB // TJ)))
                if not last:
                    load_s(g + 1, 1 - n)
                sync.dma_start(res, x_v[g]).then_inc(res_loaded, 16)
                tiles(g, TILES // 2, TILES)

            group(0, 0, first=True)
            with sync.Fori(0, GROUPS // 2 - 1) as u:
                g = 2 * u + 1
                group(g, 1)
                group(g + 1, 0)
            group(GROUPS - 1, 1, last=True)
            sync.wait_ge(y_set, done(GROUPS))
            sync.dma_start(o_v[GROUPS - 1], y).then_inc(stored, 16)
            sync.wait_ge(stored, 16 * done(GROUPS))

        @block.gpsimd
        def _(pool):
            pool.sem_inc(converted, LEAD)
            nc.gpsimd.memset(a_blk[:, :], 0.0)
            nc.gpsimd.memset(zeros[:, :], 0.0)
            nc.gpsimd.memset(eps_t[:, :], EPS)
            nc.gpsimd.memset(half_t[:, :], -0.5)
            nc.gpsimd.memset(identb[:, :], 0.0)
            nc.gpsimd.memset(identf, 0.0).then_inc(consts_set, 1)
            pool.wait_ge(consts_set, 1)
            nc.gpsimd.affine_select(out=identb[:, :], in_=identb[:, :], compare_op=ALU.not_equal, fill=1.0,
                                    base=0, pattern=[[-1, P]], channel_multiplier=1).then_inc(consts_set, 1)
            nc.gpsimd.affine_select(out=identf, in_=identf, compare_op=ALU.not_equal, fill=1.0,
                                    base=0, pattern=[[-1, P]], channel_multiplier=1).then_inc(consts_set, 1)

            pool.wait_ge(d_part_set, 1)
            nc.gpsimd.partition_all_reduce(d_max[:, :], d_part[:, :], P, bass.bass_isa.ReduceOp.max).then_inc(d_max_set, 1)
            pool.wait_ge(d_part_set, 2)
            nc.gpsimd.partition_all_reduce(wh_big[:, 1:2], wh_big[:, 0:1], P, bass.bass_isa.ReduceOp.max).then_inc(d_max_set, 1)

            with pool.Fori(0, JB // TJ // 2) as u:
                m = 2 * u
                for n in range(2):
                    pool.wait_ge(part_set, done(3 * m + n + 3))
                    nc.gpsimd.tensor_tensor(wide[:, n, :, :, 0], wide[:, n, :, :, 0], G[:, bass.ds((m + n) * TJ, TJ), :, 1, :],
                                            ALU.subtract).then_inc(rest2_set, 1)

            def convert(t, n, pair, first=False):
                pool.wait_ge(adj_loaded[n], 16 * pair + 16)
                if not first:
                    pool.wait_ge(transposed, (t - 1) * TJ)
                pool.sem_inc(begun, 1)
                nc.gpsimd.tensor_copy(conv[:, n], adj_t[:, n]).then_inc(converted, 1)

            def pairs(g, lo, hi):
                with pool.Fori(lo, hi) as c:
                    for n in range(2):
                        pair = g * (TILES // 2) + c
                        convert(2 * pair + n, n, pair)

            for n in range(2):
                convert(n, n, 0, first=True)

            def inverse_deviation(g):
                pool.wait_ge(var_set, g + 1)
                nc.gpsimd.tensor_tensor(rstd[:, :], mv[:, :, 1], half_t[:, :], ALU.pow).then_inc(rstd_set, 1)

            pairs(0, 1, TILES // 2)
            with pool.Fori(1, GROUPS) as g:
                pairs(g, 0, 2)
                inverse_deviation(g - 1)
                pairs(g, 2, TILES // 2)
            inverse_deviation(GROUPS - 1)

        @block.scalar
        def _(act):
            for ready in (step_set, part_set, xT_copied, s_copied, acc_act):
                act.sem_inc(ready, LEAD)
            act.wait_ge(wT_psum, 1)
            nc.scalar.copy(proj, sp[0][:, 0:PC]).then_inc(proj_set, 1)
            with act.Fori(0, XT // 2) as u:
                t = 2 * u
                for n in range(2):
                    act.wait_ge(xT_psum, t + n + 1)
                    if n == 0:
                        act.wait_ge(wh_psum, done(t))
                    nc.scalar.copy(xT[:, n], tr[n][:, :]).then_inc(xT_copied, 1)
                for n in range(2):
                    act.wait_ge(wh_psum, done(t + n + 1))
                    act.wait_ge(s_stored, 16 * done(t))
                    nc.scalar.copy(s_row[:, n], sp[n][0:HEADS, :]).then_inc(s_copied, 1)

            act.wait_ge(args_set, 1)
            nc.scalar.activation(Bv[:, :, :], Bv[:, :, :], ACT.Exp)
            nc.scalar.activation(Fv[:, :, :], Fv[:, :, :], ACT.Exp, scale=SLOPE)
            nc.scalar.activation(alpha[:, :, :], alpha[:, :, :], ACT.Exp)
            nc.scalar.activation(beta[:, :, :], beta[:, :, :], ACT.Exp).then_inc(exps_set, 1)

            with act.Fori(0, JB // TJ // 2) as u:
                m = 2 * u
                for part, ready in ((0, wide_set), (1, rest1_set), (2, rest2_set)):
                    for n in range(2):
                        act.wait_ge(ready, m + n + 1)
                        blk = bass.ds((m + n) * TJ, TJ)
                        last = nc.scalar.copy(G[:, blk, :, part, :], wide[:, n, :, :, 0])
                        if part == 0:
                            last = nc.scalar.activation(F[:, blk, :, 0, :], wide[:, n, :, :, 1], ACT.Copy,
                                                        scale=sigma[:, 0:1])
                        last.then_inc(part_set, 1)

            def octet(g, o, n, after_first=None):
                nth = counts(act, g * JB + o * OCT, OCT)
                act.wait_ge(step_set, nth[0] + (LEAD - 1))
                nc.scalar.copy(d_act[:, :, :], d_steep[:, bass.ds(o * OCT, OCT), 0:ACT_HEADS]).then_inc(d_act_set, 1)
                act.wait_ge(d_act_set, g * OCTS + o + 1)
                for k in range(OCT):
                    act.wait_ge(T_act, nth[k])
                    for h in range(ACT_HEADS):
                        last = nc.scalar.activation(step[:, k % 2, h], s_all[:, n, h], ACT.Sigmoid, scale=STEEP,
                                                    bias=d_act[:, k, h:h + 1])
                    last.then_inc(step_set, 1)
                    if k == 0 and after_first is not None:
                        take_sums(after_first)

            def take_sums(g):
                act.wait_ge(acc_done, g + 1)
                act.wait_ge(y_set, done(g))
                for b in range(BANKS // 2, BANKS):
                    n_ch = chunks_of(b)
                    nc.scalar.copy(late[:, b * USED:b * USED + n_ch * CH], acc[b][:, 0:n_ch * CH]).then_inc(acc_act, 1)

            def group(g, n, first=False):
                act.wait_ge(s_loaded[n], 8 * (g + 2 - n))
                octet(g, 0, n, None if first else g - 1)
                with act.Fori(1, OCTS) as o:
                    octet(g, o, n)

            group(0, 0, first=True)
            with act.Fori(0, GROUPS // 2 - 1) as u:
                g = 2 * u + 1
                group(g, 1)
                group(g + 1, 0)
            group(GROUPS - 1, 1)
            take_sums(GROUPS - 1)

        @block.vector
        def _(dve):
            links = [0]

            def link(ins):
                links[0] += 1
                ins.then_inc(dve_chain, 1)
                return links[0]

            for ready in (T_act, T_dve, wh_copied, acc_dve, y_set):
                dve.sem_inc(ready, LEAD)

            with dve.Fori(0, XT // 2) as u:
                t = 2 * u
                for n in range(2):
                    dve.wait_ge(wh_psum, done(t + n + 1))
                    for half in range(2):
                        src = acc[2 * n + half][:, 0:2 * PC].rearrange("p (b c) -> p b c", b=2)
                        blk = bass.ds((t + n) * IB + 2 * half, 2)
                        nc.vector.tensor_copy(Wh[:, blk, :], src[:, :, 0:D_ALL])
                        nc.vector.tensor_reduce(wh_part[:, bass.ds(2 * (t + n) + half, 1)], src[:, :, 0:D_ALL], AX.XY,
                                                ALU.max, apply_absolute_value=True)
                        nc.vector.tensor_copy(sd[:, blk, :], src[:, :, D_ALL:PC]).then_inc(wh_copied, 1)
            dve.wait_ge(wh_copied, done(2 * XT))
            s_c, d_c = sd[:, :, 0:HEADS], sd[:, :, HEADS:2 * HEADS]
            nc.vector.tensor_reduce(d_part[:, :], d_c.rearrange("p j h -> p h j"), AX.X, ALU.max).then_inc(d_part_set, 1)
            dve.wait_ge(dve_chain, link(nc.vector.tensor_reduce(wh_big[:, 0:1], wh_part[:, :], AX.X, ALU.max)))
            nc.vector.tensor_scalar(wh_big[:, 0:1], wh_big[:, 0:1], 1.0, None, ALU.max).then_inc(d_part_set, 1)
            dve.wait_ge(d_max_set, 1)
            D_b = d_max[:, :].unsqueeze(1).to_broadcast([P, JB, HEADS])
            nc.vector.tensor_tensor(Bv[:, :, :], d_c, D_b, ALU.subtract)
            nc.vector.tensor_tensor(Fv[:, :, :], d_c, D_b, ALU.subtract)
            dve.wait_ge(dve_chain, link(nc.vector.tensor_tensor(alpha[:, :, :], s_c, D_b, ALU.add)))
            dve.wait_ge(dve_chain, link(nc.vector.scalar_tensor_tensor(
                beta[:, :, :], alpha[:, :, :], SLOPE, alpha[:, :, :], ALU.mult, ALU.max)))
            zs = late[:, 0:JB * HEADS].rearrange("p (j h) -> p j h", h=HEADS)
            dve.wait_ge(dve_chain, link(nc.vector.tensor_tensor(zs, alpha[:, :, :], beta[:, :, :], ALU.subtract)))
            dve.wait_ge(dve_chain, link(nc.vector.scalar_tensor_tensor(
                beta[:, :, :], alpha[:, :, :], SLOPE, beta[:, :, :], ALU.mult, ALU.subtract)))
            dve.wait_ge(dve_chain, link(nc.vector.tensor_scalar(d_steep, d_neg, STEEP, None, ALU.mult)))
            nc.vector.tensor_scalar(d_neg, d_neg, -1.0, None, ALU.mult)
            nc.vector.tensor_copy(alpha[:, :, :], zs).then_inc(args_set, 1)
            dve.wait_ge(d_max_set, 2)
            dve.wait_ge(dve_chain, link(nc.vector.tensor_scalar(
                sigma[:, 0:1].bitcast(i32), wh_big[:, 1:2].bitcast(i32), EXPONENT_BITS, None, ALU.bitwise_and)))
            dve.wait_ge(dve_chain, link(nc.vector.tensor_scalar(sigma[:, 1:2], sigma[:, 0:1], 2.0 ** -14, None, ALU.mult)))
            dve.wait_ge(dve_chain, link(nc.vector.reciprocal(sigma[:, 0:1], sigma[:, 1:2])))
            dve.wait_ge(exps_set, 1)
            nc.vector.tensor_scalar(beta[:, :, :], beta[:, :, :], sigma[:, 1:2], -1.0, ALU.mult, ALU.mult)

            def weigh(m, n):
                blk = bass.ds((m + n) * TJ, TJ)
                wh = Wh[:, blk, :].rearrange("p j (h c) -> p j h c", h=HEADS)
                for k, v in enumerate((Bv, Fv)):
                    vb = v[:, blk, :]
                    nc.vector.tensor_copy(wide[:, n, :, :, k, D_OUT], vb)
                    last = nc.vector.tensor_tensor(wide[:, n, :, :, k, 0:D_OUT], wh,
                                                   vb.unsqueeze(3).to_broadcast([P, TJ, HEADS, D_OUT]), ALU.mult)
                last.then_inc(wide_set, 1)

            dve.wait_ge(args_set, 1)
            with dve.Fori(0, JB // TJ // 2) as u:
                m = 2 * u
                dve.wait_ge(part_set, done(3 * m))
                for n in range(2):
                    weigh(m, n)
                for n in range(2):
                    dve.wait_ge(part_set, done(3 * m + n + 1))
                    blk = bass.ds((m + n) * TJ, TJ)
                    for t in range(TJ):
                        last = nc.vector.scalar_tensor_tensor(
                            F[:, (m + n) * TJ + t, :, 1, :], wide[:, n, t, :, 1], sigma[:, 0:1],
                            F[:, (m + n) * TJ + t, :, 0, :], ALU.mult, ALU.subtract)
                    last.then_inc(f_set, 1)
                    nc.vector.tensor_tensor(wide[:, n, :, :, 0], wide[:, n, :, :, 0], G[:, blk, :, 0, :],
                                            ALU.subtract).then_inc(rest1_set, 1)
            dve.wait_ge(f_set, JB // TJ)
            nc.vector.tensor_scalar(M[:, :, :, :, :], F[:, :, :, :, :], -1.0, None, ALU.mult).then_inc(m_set, 1)

            def take_mask(k, nth):
                dve.wait_ge(transposed, nth)
                nc.vector.tensor_scalar(mask[:, k % NM], trb[k % 2][:, 0:ROWS], 0.0, None,
                                        ALU.not_equal).then_inc(mask_set, 1)

            def octet(g, o, n, ahead=True):
                nth = counts(dve, g * JB + o * OCT, OCT + 1)
                dve.wait_ge(T_dve, nth[0] + (LEAD - 1))
                nc.vector.tensor_copy(d_dve[:, :, :], d_neg[:, bass.ds(o * OCT, OCT), ACT_HEADS:HEADS]).then_inc(d_dve_set, 1)
                dve.wait_ge(d_dve_set, g * OCTS + o + 1)
                for k in range(OCT):
                    b = k % 2
                    dve.wait_ge(mask_set, nth[k])
                    dve.wait_ge(early_done, nth[k])
                    for h in range(ACT_HEADS, HEADS):
                        last = nc.vector.scalar_tensor_tensor(
                            T[:, b, h], s_all[:, n, h], d_dve[:, k, h - ACT_HEADS:h - ACT_HEADS + 1],
                            mask[:, k % NM], ALU.is_ge, ALU.mult)
                    last.then_inc(T_dve, 1)
                    if k + 1 < OCT or ahead:
                        take_mask(k + 1, nth[k + 1])
                    dve.wait_ge(block_done, nth[k])
                    dve.wait_ge(step_set, nth[k] + LEAD)
                    nc.vector.tensor_tensor(T[:, b, 0:ACT_HEADS], step[:, b],
                                            mask[:, k % NM].unsqueeze(1).to_broadcast([P, ACT_HEADS, ROWS]),
                                            ALU.mult).then_inc(T_act, 1)
                    yield

            def finish(g):
                got = [0]

                def wait_last(ins):
                    got[0] += 1
                    ins.then_inc(dve_chain, 1)
                    dve.wait_ge(dve_chain, CHAIN0 + g * CHAIN_STEP + got[0])

                rows = bass.ds(g * IB, IB)

                def per_row(v, width):
                    return v.rearrange("p b h -> p (b h)").unsqueeze(2).to_broadcast([P, CHUNKS, width])

                top, low = acc_sb[:, :, 0:HC], acc_sb[:, :, BC:BC + HC]
                dve.wait_ge(acc_act, done((g + 1) * (BANKS - BANKS // 2)))
                dve.wait_ge(acc_dve, done((g + 1) * (BANKS // 2)))
                nc.vector.tensor_tensor(low, low, acc_sb[:, :, BC + HC:CH], ALU.add)
                wait_last(nc.vector.tensor_tensor(top, top, acc_sb[:, :, HC:2 * HC], ALU.add))
                yield
                wait_last(nc.vector.tensor_tensor(top, top, acc_sb[:, :, 2 * HC:BC], ALU.add))
                yield
                nc.vector.tensor_tensor(low, low, per_row(beta[:, rows, :], HC), ALU.mult)
                wait_last(nc.vector.tensor_tensor(top, top, per_row(alpha[:, rows, :], HC), ALU.mult))
                yield
                wait_last(nc.vector.tensor_tensor(top, top, low, ALU.add))
                yield
                wait_last(nc.vector.tensor_scalar(rden[:, :, :], top[:, :, D_OUT].rearrange("p (b h) -> p b h", h=HEADS),
                                                  TINY, None, ALU.max))
                wait_last(nc.vector.reciprocal(rden[:, :, :], rden[:, :, :]))
                dve.wait_ge(stored, 16 * done(g))
                wait_last(nc.vector.tensor_tensor(y.rearrange("p b (h c) -> p (b h) c", h=HEADS), top[:, :, 0:D_OUT],
                                                  per_row(rden[:, :, :], D_OUT), ALU.mult))
                yield
                dve.wait_ge(res_loaded, 16 * g + 16)
                wait_last(nc.vector.tensor_tensor(y, y, res, ALU.add))
                yield
                for b in range(IB):
                    last = nc.vector.bn_stats(stats[:, b], y[:, b])
                wait_last(last)
                yield
                for b in range(IB):
                    last = nc.vector.bn_aggr(mv[:, b], stats[:, b])
                wait_last(last)
                nc.vector.tensor_scalar(mv[:, :, 1], mv[:, :, 1], EPS, None, ALU.add).then_inc(var_set, 1)
                yield
                yield
                dve.wait_ge(rstd_set, g + 1)
                for b in range(IB):
                    last = nc.vector.tensor_scalar(y[:, b], y[:, b], mv[:, b, 0:1], rstd[:, b:b + 1],
                                                   ALU.subtract, ALU.mult)
                last.then_inc(y_set, 1)

            CHAIN0, CHAIN_STEP = links[0], 10

            def take_sums(g):
                dve.wait_ge(acc_done, g + 1)
                for b in range(BANKS // 2):
                    nc.vector.tensor_copy(late[:, b * USED:(b + 1) * USED], acc[b][:, 0:USED]).then_inc(acc_dve, 1)

            def group(g, n, first=False, last=False):
                dve.wait_ge(s_loaded[n], 8 * (g + 2 - n))
                steps = octet(g, 0, n)
                next(steps)
                if first:
                    for _ in steps:
                        pass
                else:
                    take_sums(g - 1)
                    closing = finish(g - 1)
                    for steps in (steps, octet(g, 1, n)):
                        for _ in steps:
                            next(closing, None)
                    for _ in closing:
                        pass
                with dve.Fori(1 if first else 2, OCTS - last) as o:
                    for _ in octet(g, o, n):
                        pass
                if last:
                    for _ in octet(g, OCTS - 1, n, ahead=False):
                        pass

            take_mask(0, 1)
            group(0, 0, first=True)
            with dve.Fori(0, GROUPS // 2 - 1) as u:
                g = 2 * u + 1
                group(g, 1)
                group(g + 1, 0)
            group(GROUPS - 1, 1, last=True)
            take_sums(GROUPS - 1)
            for _ in finish(GROUPS - 1):
                pass

        @block.tensor
        def _(pe):
            for ready in (early_done, block_done, wh_psum):
                pe.sem_inc(ready, LEAD)
            pe.wait_ge(consts_set, 3)
            pe.wait_ge(w_loaded, 16 * (1 + 2 * HEADS))
            nc.tensor.transpose(sp[0][:, 0:P], w_sb, identf)
            nc.tensor.matmul(sp[0][:, P:PC], w_sb, a_blk[:, :], start=True, stop=True).then_inc(wT_psum, 1)
            pe.wait_ge(proj_set, 1)

            with pe.Fori(0, XT // 2) as u:
                t = 2 * u
                for n in range(2):
                    pe.wait_ge(x_loaded[n], 8 * t + 16)
                    pe.wait_ge(xT_copied, done(t))
                    for b in range(IB):
                        last = nc.tensor.transpose(tr[n][:, b * P:(b + 1) * P], xr[:, n, b], identf)
                    last.then_inc(xT_psum, 1)
                for n in range(2):
                    pe.wait_ge(xT_copied, done(t + n + 1))
                    if n == 0:
                        pe.wait_ge(wh_copied, done(2 * t))
                        pe.wait_ge(s_copied, done(t))
                    for b in range(IB):
                        nc.tensor.matmul(acc[2 * n + b // 2][:, (b % 2) * PC:(b % 2 + 1) * PC],
                                         xT[:, n, b * P:(b + 1) * P], proj, start=True, stop=True)
                    nc.tensor.matmul(sp[n][0:HEADS, :], proj[:, D_ALL:D_ALL + HEADS], xT[:, n],
                                     start=True, stop=True).then_inc(wh_psum, 1)

            def transpose_block(tile, k, nth=None):
                b = k % 2
                if k % TJ == 0:
                    pe.wait_ge(converted, done(tile + k // TJ + 1))
                if nth is not None:
                    pe.wait_ge(mask_set, nth[k - 2])
                for r in range(IB):
                    last = nc.tensor.transpose(trb[b][:, r * P:(r + 1) * P],
                                               conv[:, (k // TJ) % 2, r, (k % TJ) * P:(k % TJ + 1) * P], identb[:, :])
                last.then_inc(transposed, 1)

            G_flat = G_words[:, :, :].rearrange("p j c -> p (j c)")
            F_flat = F[:, :, :, :, :].rearrange("p j h s c -> p (j h s c)")
            M_flat = M[:, :, :, :, :].rearrange("p j h s c -> p (j h s c)")

            def chunk(r, h):
                n = r * HEADS + h
                return acc[n // PER_BANK], n % PER_BANK * CH

            def add_block(g_at, f_at, k, nth):
                b = k % 2

                def add(lhsT, flat, start, width, dst):
                    return nc.tensor.matmul(dst, lhsT, flat[:, bass.ds(start, width)], start=False, stop=False,
                                            skip_group_check=True)

                pe.wait_ge(mask_set, nth[k])
                for r in range(IB):
                    h = 0
                    while h < HEADS:
                        bank_h, col = chunk(r, h)
                        n = min(HEADS - h, PER_BANK - col // CH)
                        dst = bank_h[:, col:col + n * CH].rearrange("p (n c) -> p n c", c=CH)[:, :, BC:CH]
                        add(mask[:, k % NM, r * P:(r + 1) * P], M_flat, f_at + (k * HEADS + h) * FC, n * FC, dst)
                        h += n
                for heads, ready, free in ((range(ACT_HEADS, HEADS), T_dve, early_done),
                                           (range(ACT_HEADS), T_act, block_done)):
                    pe.wait_ge(ready, nth[k] + LEAD)
                    for h in heads:
                        for flat, at, width, first in ((G_flat, g_at, BC, 0), (F_flat, f_at, FC, BC)):
                            for r in range(IB):
                                bank_h, col = chunk(r, h)
                                last = add(T[:, b, h, r * P:(r + 1) * P], flat, at + (k * HEADS + h) * width, width,
                                           bank_h[:, col + first:col + first + width])
                    last.then_inc(free, 1)

            def octet(g, o, ahead):
                nth = counts(pe, g * JB + o * OCT, OCT)
                tile = g * TILES + o * (OCT // TJ)
                g_at, f_at = o * (OCT * HEADS * BC), o * (OCT * HEADS * FC)
                if not isinstance(o, int):
                    g_at, f_at = pe.snap(g_at), pe.snap(f_at)
                for k in range(OCT):
                    if k + 2 < OCT or ahead:
                        transpose_block(tile, k + 2, nth)
                    add_block(g_at, f_at, k, nth)

            def open_sums(g):
                pe.wait_ge(acc_dve, done(g * (BANKS // 2)))
                pe.wait_ge(acc_act, done(g * (BANKS - BANKS // 2)))
                for b in range(BANKS):
                    nc.tensor.matmul(acc[b][:, USED:USED + 2], identb[:, :], zeros[:, :], start=True, stop=False,
                                     skip_group_check=True)

            def close_sums():
                for b in range(BANKS):
                    last = nc.tensor.matmul(acc[b][:, USED:USED + 2], identb[:, :], zeros[:, :], start=False, stop=True,
                                            skip_group_check=True)
                last.then_inc(acc_done, 1)

            pe.wait_ge(m_set, 1)
            pe.wait_ge(part_set, done(3 * (JB // TJ)))
            pe.wait_ge(s_copied, done(XT))
            for k in range(2):
                transpose_block(0, k)
            with pe.Fori(0, GROUPS - 1) as g:
                open_sums(g)
                with pe.Fori(0, OCTS) as o:
                    octet(g, o, True)
                close_sums()
            open_sums(GROUPS - 1)
            with pe.Fori(0, OCTS - 1) as o:
                octet(GROUPS - 1, o, True)
            octet(GROUPS - 1, OCTS - 1, False)
            close_sums()


_INS = ["x", "adj", "L0_gnn_W", "L0_gnn_a"]


def kernel(**inputs):
    import numpy as np
    import concourse.bacc as bacc
    from concourse.bass_utils import run_bass_kernel_spmd

    nc = bacc.Bacc("TRN2", target_bir_lowering=False, num_devices=1)
    arrays, args = {}, []
    for name in _INS:
        v = np.ascontiguousarray(inputs[name])
        arrays[f"in_{name}"] = v
        args.append(nc.dram_tensor(f"in_{name}", v.shape, mybir.dt.from_np(v.dtype), kind="ExternalInput").ap())
    shape = inputs["x"].shape
    args.append(nc.dram_tensor("out", shape, mybir.dt.float32, kind="ExternalOutput").ap())
    gat_layernorm(nc, *args)
    r = run_bass_kernel_spmd(nc, [arrays], core_ids=[0])
    return r.results[0]["out"]
```

```python
from contextlib import ExitStack

import concourse.bass as bass
from concourse import mybir


def gat_layernorm(nc, x, adj, W, a, out):
    fp32, bf16, fp16, i32 = mybir.dt.float32, mybir.dt.bfloat16, mybir.dt.float16, mybir.dt.int32
    ALU = mybir.AluOpType
    ACT = mybir.ActivationFunctionType
    AX = mybir.AxisListType

    P = 128
    N, D_IN = x.shape
    HEADS, D_OUT = a.shape[0], a.shape[1] // 2
    D_ALL = HEADS * D_OUT
    SLOPE, EPS = 0.2, 1e-5
    STEEP = 2.0 ** 40
    EXPONENT_BITS = 0x7F800000
    TINY = 1e-37

    IB = 4
    ROWS = IB * P
    GROUPS = N // ROWS
    JB = N // P
    TJ = 4
    NW = 4
    OCT = 8
    OCTS = JB // OCT
    XT = N // ROWS

    NB = 4
    NM = 2 * NB
    HC = D_OUT + 1
    BP, FP = 3, 2
    BC, FC = BP * HC, FP * HC
    CH = BC + FC
    CHUNKS = IB * HEADS
    PER_BANK = 512 // CH
    BANKS = -(-CHUNKS // PER_BANK)
    USED = PER_BANK * CH
    ACT_HEADS = 3
    POOL_HEAD = 0
    DVE_HEAD = 3
    PC = D_ALL + 2 * HEADS

    ctx = ExitStack()
    with ctx:
        def sb(name, shape, dt):
            return ctx.enter_context(nc.sbuf_tensor(name, shape, dt))

        def sem(name):
            return ctx.enter_context(nc.semaphore(name))

        G_words = sb("G", [P, JB, HEADS * BC], bf16)
        G = G_words[:, :, :].rearrange("p j (h s c) -> p j h s c", h=HEADS, s=BP)
        F = sb("F", [P, JB, HEADS, FP, HC], fp16)
        M = sb("M", [P, JB, HEADS, FP, HC], fp16)
        s_all = sb("s_all", [P, 2, HEADS, ROWS], fp32)
        adj_t = sb("adj_t", [P, 2, IB, OCT * P], bf16)
        mask = sb("mask", [P, NM, ROWS], bf16)
        step = sb("step", [P, NB, ACT_HEADS, ROWS], bf16)
        T = sb("T", [P, NB, HEADS, ROWS], bf16)
        xr = sb("xr", [P, 2, IB, D_IN], fp32)
        res, y = xr[:, 0], xr[:, 1]
        T_words = T[:, :, :, :].rearrange("p n h r -> p (n h r)").bitcast(fp32)
        w_sb, identf, proj = T_words[:, 0:D_IN], T_words[:, D_IN:D_IN + P], T_words[:, D_IN + P:D_IN + P + PC]
        a_blk = sb("a_blk", [P, 2 * HEADS], fp32)
        identb = sb("identb", [P, P], bf16)
        zeros = sb("zeros", [P, 2], bf16)
        d_act = sb("d_act", [P, OCT, ACT_HEADS], fp32)
        d_dve = sb("d_dve", [P, OCT], fp32)
        s_row = T_words[0:HEADS, D_IN + P + PC:D_IN + P + PC + 2 * ROWS].rearrange("p (n r) -> p n r", n=2)
        sd = sb("sd", [P, JB, 2 * HEADS], fp32)
        d_steep, d_neg = sd[:, :, 0:HEADS], sd[:, :, HEADS:2 * HEADS]
        Bv, Fv = (s_all[:, 1, h, 0:JB * HEADS].rearrange("p (j h) -> p j h", h=HEADS) for h in range(2))
        alpha = sb("alpha", [P, JB, HEADS], fp32)
        beta = sb("beta", [P, JB, HEADS], fp32)
        d_part = sb("d_part", [P, HEADS], fp32)
        d_max = sb("d_max", [P, HEADS], fp32)
        wh_part = sb("wh_part", [P, 2 * XT], fp32)
        wh_big = sb("wh_big", [P, 2], fp32)
        sigma = sb("sigma", [P, 2], fp32)
        late = sb("late", [P, CHUNKS * CH], fp32)
        WIDE = TJ * HEADS * 2 * HC
        in_T = D_IN + P + PC + 2 * ROWS
        wide = [part.rearrange("p (t h k c) -> p t h k c", t=TJ, h=HEADS, k=2)
                for start, words in ((0, late), (in_T, T_words))
                for part in (words[:, start + n * WIDE:start + (n + 1) * WIDE] for n in range(NW // 2))]
        xT = late[:, 0:2 * ROWS].rearrange("p (n r) -> p n r", n=2)
        acc_sb = late[:, :].rearrange("p (k c) -> p k c", c=CH)
        rden = sb("rden", [P, IB, HEADS], fp32)
        stats = sb("stats", [P, IB, 6], fp32)
        mv = sb("mv", [P, IB, 2], fp32)
        rstd = sb("rstd", [P, IB], fp32)
        minus_half = sb("minus_half", [P, IB], fp32)
        Wh = G_words[:, :, :].bitcast(fp32)[:, :, 0:D_ALL]

        bank = [ctx.enter_context(nc.psum_tensor(f"bank{n}", [P, 512], fp32)) for n in range(8)]
        acc, tr, sp = bank[0:BANKS], bank[BANKS:8], bank[BANKS - 2:BANKS]
        trb = [t[:, :].bitcast(bf16) for t in tr]

        sT = nc.dram_tensor("sT_scratch", [HEADS, N], fp32, kind="Internal").ap()

        x_v = x.rearrange("(t b p) f -> t p b f", b=IB, p=P)
        o_v = out.rearrange("(t b p) f -> t p b f", b=IB, p=P)
        adj_v = adj.rearrange("(g b p) (c n) -> g c p b n", b=IB, p=P, n=OCT * P)
        sT_v = sT.rearrange("h (t n) -> t h n", n=ROWS)

        consts_set = sem("consts_set")
        w_loaded = sem("w_loaded")
        x_loaded = [sem(f"x_loaded{n}") for n in range(2)]
        xT_psum = sem("xT_psum")
        xT_copied = sem("xT_copied")
        wT_psum = sem("wT_psum")
        proj_set = sem("proj_set")
        wh_psum = sem("wh_psum")
        wh_copied = sem("wh_copied")
        s_copied = sem("s_copied")
        s_stored = sem("s_stored")
        s_loaded = [sem(f"s_loaded{n}") for n in range(2)]
        d_part_set = sem("d_part_set")
        d_max_set = sem("d_max_set")
        args_set = sem("args_set")
        exps_set = sem("exps_set")
        wide_set = sem("wide_set")
        part_set = sem("part_set")
        f_set = sem("f_set")
        m_set = sem("m_set")
        rest1_set = sem("rest1_set")
        rest2_set = sem("rest2_set")
        adj_loaded = [sem(f"adj_loaded{n}") for n in range(2)]
        transposed = sem("transposed")
        mask_set = sem("mask_set")
        step_pool_set = sem("step_pool_set")
        step_set = sem("step_set")
        d_act_set = sem("d_act_set")
        d_dve_set = sem("d_dve_set")
        T_dve = sem("T_dve")
        T_act = sem("T_act")
        T_pool = sem("T_pool")
        early_done = sem("early_done")
        block_done = sem("block_done")
        acc_done = sem("acc_done")
        acc_dve = sem("acc_dve")
        acc_act = sem("acc_act")
        res_loaded = sem("res_loaded")
        var_set = sem("var_set")
        rstd_set = sem("rstd_set")
        y_set = sem("y_set")
        stored = sem("stored")
        dve_chain = sem("dve_chain")

        def chunks_of(b):
            return min(PER_BANK, CHUNKS - b * PER_BANK)

        def counts(eng, q, n):
            return [q + k + 1 if isinstance(q, int) else eng.snap(q + k + 1) for k in range(n)]

        block = ctx.enter_context(nc.Block())

        LEAD = NB

        def done(n):
            return n + LEAD

        @block.sync
        def _(sync):
            sync.sem_inc(stored, 16 * LEAD)
            sync.sem_inc(s_stored, 16 * LEAD)
            sync.dma_start(w_sb, W[:, :]).then_inc(w_loaded, 16)
            sync.wait_ge(consts_set, 1)
            for h in range(HEADS):
                for side in range(2):
                    sync.dma_start(a_blk[h * D_OUT:(h + 1) * D_OUT, side * HEADS + h:side * HEADS + h + 1],
                                   a[h:h + 1, side * D_OUT:(side + 1) * D_OUT].rearrange("o n -> n o")
                                   ).then_inc(w_loaded, 16)

            def x_tile(t, n, waits):
                if waits:
                    sync.wait_ge(xT_psum, t - 1)
                sync.dma_start(xr[:, n], x_v[t]).then_inc(x_loaded[n], 16)

            def s_store(t, n):
                sync.wait_ge(s_copied, done(t + 1))
                sync.dma_start(sT_v[t], s_row[:, n]).then_inc(s_stored, 16)

            x_tile(0, 0, False)
            x_tile(1, 1, False)

            with sync.Fori(0, XT // 2 - 1) as u:
                t = 2 * u
                for n in range(2):
                    x_tile(t + n + 2, n, True)
                    s_store(t + n, n)
            for n in range(2):
                s_store(XT - 2 + n, n)
            sync.wait_ge(s_stored, 16 * done(XT))

            def load_s(g, n):
                src = sT_v[g].unsqueeze(0).to_broadcast([P, HEADS, ROWS])
                sync.dma_start(s_all[:, n], src).then_inc(s_loaded[n], 16)

            load_s(0, 0)

            def group(g, n, first=False, last=False):
                if not first:
                    sync.wait_ge(y_set, done(g))
                    sync.dma_start(o_v[g - 1], y).then_inc(stored, 16)
                else:
                    sync.wait_ge(part_set, done(3 * (JB // TJ)))
                if not last:
                    load_s(g + 1, 1 - n)
                sync.dma_start(res, x_v[g]).then_inc(res_loaded, 16)

            group(0, 0, first=True)
            with sync.Fori(0, GROUPS // 2 - 1) as u:
                g = 2 * u + 1
                group(g, 1)
                group(g + 1, 0)
            group(GROUPS - 1, 1, last=True)
            sync.wait_ge(y_set, done(GROUPS))
            sync.dma_start(o_v[GROUPS - 1], y).then_inc(stored, 16)
            sync.wait_ge(stored, 16 * done(GROUPS))

        @block.gpsimd
        def _(pool):
            pool.sem_inc(T_pool, LEAD)
            for n in range(2):
                nc.gpsimd.dma_start(adj_t[:, n], adj_v[0, n]).then_inc(adj_loaded[n], 16)
            nc.gpsimd.memset(a_blk[:, :], 0.0)
            nc.gpsimd.memset(zeros[:, :], 0.0)
            nc.gpsimd.memset(minus_half[:, :], -0.5)
            nc.gpsimd.memset(identb[:, :], 0.0)
            nc.gpsimd.memset(identf, 0.0).then_inc(consts_set, 1)
            pool.wait_ge(consts_set, 1)
            nc.gpsimd.affine_select(out=identb[:, :], in_=identb[:, :], compare_op=ALU.not_equal, fill=1.0,
                                    base=0, pattern=[[-1, P]], channel_multiplier=1).then_inc(consts_set, 1)
            nc.gpsimd.affine_select(out=identf, in_=identf, compare_op=ALU.not_equal, fill=1.0,
                                    base=0, pattern=[[-1, P]], channel_multiplier=1).then_inc(consts_set, 1)

            pool.wait_ge(d_part_set, 1)
            nc.gpsimd.partition_all_reduce(d_max[:, :], d_part[:, :], P, bass.bass_isa.ReduceOp.max).then_inc(d_max_set, 1)
            pool.wait_ge(d_part_set, 2)
            nc.gpsimd.partition_all_reduce(wh_big[:, 1:2], wh_big[:, 0:1], P, bass.bass_isa.ReduceOp.max).then_inc(d_max_set, 1)

            with pool.Fori(0, JB // TJ // NW) as u:
                m = NW * u
                for n in range(NW):
                    pool.wait_ge(part_set, done(3 * m + NW + n + 1))
                    nc.gpsimd.tensor_tensor(wide[n][:, :, :, 0], wide[n][:, :, :, 0], G[:, bass.ds((m + n) * TJ, TJ), :, 1, :],
                                            ALU.subtract).then_inc(rest2_set, 1)

            def load_tile(g, c, t, n):
                pool.wait_ge(transposed, (t - 1) * OCT)
                nc.gpsimd.dma_start(adj_t[:, n], adj_v[g, c]).then_inc(adj_loaded[n], 16)

            def inverse_deviation(g):
                pool.wait_ge(var_set, g + 1)
                nc.gpsimd.tensor_tensor(rstd[:, :], mv[:, :, 1], minus_half[:, :], ALU.pow).then_inc(rstd_set, 1)

            def octet(g, o, half, load=True, next_group=False, rstd_of=None):
                if load:
                    g_next, o_next = (g + 1, 0) if next_group else (g, o + 1)
                    load_tile(g_next, o_next, g * OCTS + o + 1, 1 - half)
                nth = counts(pool, g * JB + o * OCT, OCT)
                for k in range(OCT):
                    pool.wait_ge(mask_set, nth[k])
                    pool.wait_ge(early_done, nth[k])
                    pool.wait_ge(step_pool_set, nth[k])
                    nc.gpsimd.tensor_tensor(T[:, k % NB, POOL_HEAD], step[:, k % NB, POOL_HEAD], mask[:, k % NM],
                                            ALU.mult).then_inc(T_pool, 1)
                    if k == 1 and rstd_of is not None:
                        inverse_deviation(rstd_of)

            def group(g, first=False, last=False):
                octet(g, 0, 0, load=not first)
                octet(g, 1, 1, rstd_of=None if first else g - 1)
                with pool.Fori(1, OCTS // 2 - 1) as u:
                    for half in range(2):
                        octet(g, 2 * u + half, half)
                octet(g, OCTS - 2, 0)
                octet(g, OCTS - 1, 1, load=not last, next_group=True)

            group(0, first=True)
            with pool.Fori(1, GROUPS - 1) as g:
                group(g)
            group(GROUPS - 1, last=True)
            inverse_deviation(GROUPS - 1)

        @block.scalar
        def _(act):
            for ready in (step_set, part_set, xT_copied, s_copied, acc_act):
                act.sem_inc(ready, LEAD)
            act.wait_ge(wT_psum, 1)
            nc.scalar.copy(proj, sp[0][:, 0:PC]).then_inc(proj_set, 1)
            with act.Fori(0, XT // 2) as u:
                t = 2 * u
                for n in range(2):
                    act.wait_ge(xT_psum, t + n + 1)
                    if n == 0:
                        act.wait_ge(wh_psum, done(t))
                    nc.scalar.copy(xT[:, n], tr[n][:, :]).then_inc(xT_copied, 1)
                for n in range(2):
                    act.wait_ge(wh_psum, done(t + n + 1))
                    act.wait_ge(s_stored, 16 * done(t))
                    nc.scalar.copy(s_row[:, n], sp[n][0:HEADS, :]).then_inc(s_copied, 1)

            act.wait_ge(args_set, 1)
            nc.scalar.activation(Bv[:, :, :], Bv[:, :, :], ACT.Exp)
            nc.scalar.activation(Fv[:, :, :], Fv[:, :, :], ACT.Exp, scale=SLOPE)
            nc.scalar.activation(alpha[:, :, :], alpha[:, :, :], ACT.Exp)
            nc.scalar.activation(beta[:, :, :], beta[:, :, :], ACT.Exp).then_inc(exps_set, 1)

            with act.Fori(0, JB // TJ // NW) as u:
                m = NW * u
                for part, ready in ((0, wide_set), (1, rest1_set), (2, rest2_set)):
                    for n in range(NW):
                        act.wait_ge(ready, m + n + 1)
                        blk = bass.ds((m + n) * TJ, TJ)
                        last = nc.scalar.copy(G[:, blk, :, part, :], wide[n][:, :, :, 0])
                        if part == 0:
                            last = nc.scalar.activation(F[:, blk, :, 0, :], wide[n][:, :, :, 1], ACT.Copy,
                                                        scale=sigma[:, 0:1])
                        last.then_inc(part_set, 1)

            def octet(g, o, n, sums_of=None):
                nth = counts(act, g * JB + o * OCT, OCT)
                act.wait_ge(step_set, nth[0] + (LEAD - 1))
                nc.scalar.copy(d_act[:, :, :], d_steep[:, bass.ds(o * OCT, OCT), 0:ACT_HEADS]).then_inc(d_act_set, 1)
                act.wait_ge(d_act_set, g * OCTS + o + 1)
                for k in range(OCT):
                    act.wait_ge(T_act, nth[k])
                    act.wait_ge(T_pool, nth[k])
                    for h in range(ACT_HEADS):
                        last = nc.scalar.activation(step[:, k % NB, h], s_all[:, n, h], ACT.Sigmoid, scale=STEEP,
                                                    bias=d_act[:, k, h:h + 1])
                        if h == POOL_HEAD:
                            last.then_inc(step_pool_set, 1)
                    last.then_inc(step_set, 1)
                    if k == 0 and sums_of is not None:
                        take_sums(sums_of)

            def take_sums(g):
                act.wait_ge(acc_done, g + 1)
                act.wait_ge(y_set, done(g))
                for b in range(BANKS // 2, BANKS):
                    n_ch = chunks_of(b)
                    nc.scalar.copy(late[:, b * USED:b * USED + n_ch * CH], acc[b][:, 0:n_ch * CH]).then_inc(acc_act, 1)

            def group(g, n, first=False):
                act.wait_ge(s_loaded[n], 8 * (g + 2 - n))
                octet(g, 0, n, None if first else g - 1)
                with act.Fori(1, OCTS) as o:
                    octet(g, o, n)

            group(0, 0, first=True)
            with act.Fori(0, GROUPS // 2 - 1) as u:
                g = 2 * u + 1
                group(g, 1)
                group(g + 1, 0)
            group(GROUPS - 1, 1)
            take_sums(GROUPS - 1)

        @block.vector
        def _(dve):
            links = [0]

            def link(ins):
                links[0] += 1
                ins.then_inc(dve_chain, 1)
                return links[0]

            for ready in (T_act, T_dve, wh_copied, acc_dve, y_set):
                dve.sem_inc(ready, LEAD)

            with dve.Fori(0, XT // 2) as u:
                t = 2 * u
                for n in range(2):
                    dve.wait_ge(wh_psum, done(t + n + 1))
                    for half in range(2):
                        src = acc[2 * n + half][:, 0:2 * PC].rearrange("p (b c) -> p b c", b=2)
                        blk = bass.ds((t + n) * IB + 2 * half, 2)
                        nc.vector.tensor_copy(Wh[:, blk, :], src[:, :, 0:D_ALL])
                        nc.vector.tensor_reduce(wh_part[:, bass.ds(2 * (t + n) + half, 1)], src[:, :, 0:D_ALL], AX.XY,
                                                ALU.max, apply_absolute_value=True)
                        nc.vector.tensor_copy(sd[:, blk, :], src[:, :, D_ALL:PC]).then_inc(wh_copied, 1)
            dve.wait_ge(wh_copied, done(2 * XT))
            s_c, d_c = sd[:, :, 0:HEADS], sd[:, :, HEADS:2 * HEADS]
            nc.vector.tensor_reduce(d_part[:, :], d_c.rearrange("p j h -> p h j"), AX.X, ALU.max).then_inc(d_part_set, 1)
            dve.wait_ge(dve_chain, link(nc.vector.tensor_reduce(wh_big[:, 0:1], wh_part[:, :], AX.X, ALU.max)))
            nc.vector.tensor_scalar(wh_big[:, 0:1], wh_big[:, 0:1], 1.0, None, ALU.max).then_inc(d_part_set, 1)
            dve.wait_ge(d_max_set, 1)
            D_b = d_max[:, :].unsqueeze(1).to_broadcast([P, JB, HEADS])
            nc.vector.tensor_tensor(Bv[:, :, :], d_c, D_b, ALU.subtract)
            nc.vector.tensor_tensor(Fv[:, :, :], d_c, D_b, ALU.subtract)
            dve.wait_ge(dve_chain, link(nc.vector.tensor_tensor(alpha[:, :, :], s_c, D_b, ALU.add)))
            dve.wait_ge(dve_chain, link(nc.vector.scalar_tensor_tensor(
                beta[:, :, :], alpha[:, :, :], SLOPE, alpha[:, :, :], ALU.mult, ALU.max)))
            zs = late[:, 0:JB * HEADS].rearrange("p (j h) -> p j h", h=HEADS)
            dve.wait_ge(dve_chain, link(nc.vector.tensor_tensor(zs, alpha[:, :, :], beta[:, :, :], ALU.subtract)))
            dve.wait_ge(dve_chain, link(nc.vector.scalar_tensor_tensor(
                beta[:, :, :], alpha[:, :, :], SLOPE, beta[:, :, :], ALU.mult, ALU.subtract)))
            dve.wait_ge(dve_chain, link(nc.vector.tensor_scalar(d_steep, d_neg, STEEP, None, ALU.mult)))
            nc.vector.tensor_scalar(d_neg, d_neg, -1.0, None, ALU.mult)
            nc.vector.tensor_copy(alpha[:, :, :], zs).then_inc(args_set, 1)
            dve.wait_ge(d_max_set, 2)
            dve.wait_ge(dve_chain, link(nc.vector.tensor_scalar(
                sigma[:, 0:1].bitcast(i32), wh_big[:, 1:2].bitcast(i32), EXPONENT_BITS, None, ALU.bitwise_and)))
            dve.wait_ge(dve_chain, link(nc.vector.tensor_scalar(sigma[:, 1:2], sigma[:, 0:1], 2.0 ** -14, None, ALU.mult)))
            dve.wait_ge(dve_chain, link(nc.vector.reciprocal(sigma[:, 0:1], sigma[:, 1:2])))
            dve.wait_ge(exps_set, 1)
            nc.vector.tensor_scalar(beta[:, :, :], beta[:, :, :], sigma[:, 1:2], -1.0, ALU.mult, ALU.mult)

            def weigh(m, n):
                blk = bass.ds((m + n) * TJ, TJ)
                wh = Wh[:, blk, :].rearrange("p j (h c) -> p j h c", h=HEADS)
                for k, v in enumerate((Bv, Fv)):
                    vb = v[:, blk, :]
                    nc.vector.tensor_copy(wide[n][:, :, :, k, D_OUT], vb)
                    last = nc.vector.tensor_tensor(wide[n][:, :, :, k, 0:D_OUT], wh,
                                                   vb.unsqueeze(3).to_broadcast([P, TJ, HEADS, D_OUT]), ALU.mult)
                last.then_inc(wide_set, 1)

            dve.wait_ge(args_set, 1)
            with dve.Fori(0, JB // TJ // NW) as u:
                m = NW * u
                for n in range(NW):
                    dve.wait_ge(part_set, done(3 * m - NW + n + 1))
                    weigh(m, n)
                for n in range(NW):
                    dve.wait_ge(part_set, done(3 * m + n + 1))
                    blk = bass.ds((m + n) * TJ, TJ)
                    for t in range(TJ):
                        last = nc.vector.scalar_tensor_tensor(
                            F[:, (m + n) * TJ + t, :, 1, :], wide[n][:, t, :, 1], sigma[:, 0:1],
                            F[:, (m + n) * TJ + t, :, 0, :], ALU.mult, ALU.subtract)
                    last.then_inc(f_set, 1)
                    nc.vector.tensor_tensor(wide[n][:, :, :, 0], wide[n][:, :, :, 0], G[:, blk, :, 0, :],
                                            ALU.subtract).then_inc(rest1_set, 1)
            dve.wait_ge(f_set, JB // TJ)
            nc.vector.tensor_scalar(M[:, :, :, :, :], F[:, :, :, :, :], -1.0, None, ALU.mult).then_inc(m_set, 1)

            dve.wait_ge(part_set, done(3 * (JB // TJ)))

            def take_mask(k, nth):
                dve.wait_ge(transposed, nth)
                nc.vector.tensor_scalar(mask[:, k % NM], trb[k % 2][:, 0:ROWS], 0.0, None,
                                        ALU.not_equal).then_inc(mask_set, 1)

            def octet(g, o, n, ahead=True):
                nth = counts(dve, g * JB + o * OCT, OCT + 1)
                dve.wait_ge(T_dve, nth[0] + (LEAD - 1))
                nc.vector.tensor_copy(d_dve[:, :], d_neg[:, bass.ds(o * OCT, OCT), DVE_HEAD]).then_inc(d_dve_set, 1)
                dve.wait_ge(d_dve_set, g * OCTS + o + 1)
                for k in range(OCT):
                    b = k % NB
                    dve.wait_ge(mask_set, nth[k])
                    dve.wait_ge(early_done, nth[k])
                    nc.vector.scalar_tensor_tensor(T[:, b, DVE_HEAD], s_all[:, n, DVE_HEAD], d_dve[:, k:k + 1],
                                                   mask[:, k % NM], ALU.is_ge, ALU.mult).then_inc(T_dve, 1)
                    if k + 1 < OCT or ahead:
                        take_mask(k + 1, nth[k + 1])
                    dve.wait_ge(block_done, nth[k])
                    dve.wait_ge(step_set, nth[k] + LEAD)
                    nc.vector.tensor_tensor(T[:, b, POOL_HEAD + 1:ACT_HEADS], step[:, b, POOL_HEAD + 1:],
                                            mask[:, k % NM].unsqueeze(1).to_broadcast([P, ACT_HEADS - 1, ROWS]),
                                            ALU.mult).then_inc(T_act, 1)
                    yield

            def finish(g):
                got = [0]

                def wait_last(ins):
                    got[0] += 1
                    ins.then_inc(dve_chain, 1)
                    dve.wait_ge(dve_chain, CHAIN0 + g * CHAIN_STEP + got[0])

                rows = bass.ds(g * IB, IB)

                def per_row(v, width):
                    return v.rearrange("p b h -> p (b h)").unsqueeze(2).to_broadcast([P, CHUNKS, width])

                top, low = acc_sb[:, :, 0:HC], acc_sb[:, :, BC:BC + HC]
                dve.wait_ge(acc_act, done((g + 1) * (BANKS - BANKS // 2)))
                dve.wait_ge(acc_dve, done((g + 1) * (BANKS // 2)))
                nc.vector.tensor_tensor(low, low, acc_sb[:, :, BC + HC:CH], ALU.add)
                wait_last(nc.vector.tensor_tensor(top, top, acc_sb[:, :, HC:2 * HC], ALU.add))
                yield
                wait_last(nc.vector.tensor_tensor(top, top, acc_sb[:, :, 2 * HC:BC], ALU.add))
                yield
                nc.vector.tensor_tensor(low, low, per_row(beta[:, rows, :], HC), ALU.mult)
                wait_last(nc.vector.tensor_tensor(top, top, per_row(alpha[:, rows, :], HC), ALU.mult))
                yield
                wait_last(nc.vector.tensor_tensor(top, top, low, ALU.add))
                yield
                wait_last(nc.vector.tensor_scalar(rden[:, :, :], top[:, :, D_OUT].rearrange("p (b h) -> p b h", h=HEADS),
                                                  TINY, None, ALU.max))
                wait_last(nc.vector.reciprocal(rden[:, :, :], rden[:, :, :]))
                dve.wait_ge(stored, 16 * done(g))
                wait_last(nc.vector.tensor_tensor(y.rearrange("p b (h c) -> p (b h) c", h=HEADS), top[:, :, 0:D_OUT],
                                                  per_row(rden[:, :, :], D_OUT), ALU.mult))
                yield
                dve.wait_ge(res_loaded, 16 * g + 16)
                wait_last(nc.vector.tensor_tensor(y, y, res, ALU.add))
                yield
                for b in range(IB):
                    last = nc.vector.bn_stats(stats[:, b], y[:, b])
                wait_last(last)
                yield
                for b in range(IB):
                    last = nc.vector.bn_aggr(mv[:, b], stats[:, b])
                wait_last(last)
                nc.vector.tensor_scalar(mv[:, :, 1], mv[:, :, 1], EPS, None, ALU.add).then_inc(var_set, 1)
                yield
                yield
                dve.wait_ge(rstd_set, g + 1)
                for b in range(IB):
                    last = nc.vector.tensor_scalar(y[:, b], y[:, b], mv[:, b, 0:1], rstd[:, b:b + 1],
                                                   ALU.subtract, ALU.mult)
                last.then_inc(y_set, 1)

            CHAIN0, CHAIN_STEP = links[0], 10

            def take_sums(g):
                dve.wait_ge(acc_done, g + 1)
                for b in range(BANKS // 2):
                    nc.vector.tensor_copy(late[:, b * USED:(b + 1) * USED], acc[b][:, 0:USED]).then_inc(acc_dve, 1)

            def group(g, n, first=False, last=False):
                dve.wait_ge(s_loaded[n], 8 * (g + 2 - n))
                steps = octet(g, 0, n)
                next(steps)
                if first:
                    for _ in steps:
                        pass
                else:
                    take_sums(g - 1)
                    closing = finish(g - 1)
                    for steps in (steps, octet(g, 1, n)):
                        for _ in steps:
                            next(closing, None)
                    for _ in closing:
                        pass
                with dve.Fori(1 if first else 2, OCTS - last) as o:
                    for _ in octet(g, o, n):
                        pass
                if last:
                    for _ in octet(g, OCTS - 1, n, ahead=False):
                        pass

            take_mask(0, 1)
            group(0, 0, first=True)
            with dve.Fori(0, GROUPS // 2 - 1) as u:
                g = 2 * u + 1
                group(g, 1)
                group(g + 1, 0)
            group(GROUPS - 1, 1, last=True)
            take_sums(GROUPS - 1)
            for _ in finish(GROUPS - 1):
                pass

        @block.tensor
        def _(pe):
            for ready in (early_done, block_done, wh_psum):
                pe.sem_inc(ready, LEAD)
            pe.wait_ge(consts_set, 3)
            pe.wait_ge(w_loaded, 16 * (1 + 2 * HEADS))
            nc.tensor.transpose(sp[0][:, 0:P], w_sb, identf)
            nc.tensor.matmul(sp[0][:, P:PC], w_sb, a_blk[:, :], start=True, stop=True).then_inc(wT_psum, 1)
            pe.wait_ge(proj_set, 1)

            with pe.Fori(0, XT // 2) as u:
                t = 2 * u
                for n in range(2):
                    pe.wait_ge(x_loaded[n], 8 * t + 16)
                    pe.wait_ge(xT_copied, done(t))
                    for b in range(IB):
                        last = nc.tensor.transpose(tr[n][:, b * P:(b + 1) * P], xr[:, n, b], identf)
                    last.then_inc(xT_psum, 1)
                for n in range(2):
                    pe.wait_ge(xT_copied, done(t + n + 1))
                    if n == 0:
                        pe.wait_ge(wh_copied, done(2 * t))
                        pe.wait_ge(s_copied, done(t))
                    for b in range(IB):
                        nc.tensor.matmul(acc[2 * n + b // 2][:, (b % 2) * PC:(b % 2 + 1) * PC],
                                         xT[:, n, b * P:(b + 1) * P], proj, start=True, stop=True)
                    nc.tensor.matmul(sp[n][0:HEADS, :], proj[:, D_ALL:D_ALL + HEADS], xT[:, n],
                                     start=True, stop=True).then_inc(wh_psum, 1)

            def transpose_block(pair, half, k, nth=None):
                b = k % 2
                pair, half = (pair + 1, 0) if half and k >= OCT else (pair, half + k // OCT)
                if k % OCT == 0:
                    pe.wait_ge(adj_loaded[half], 16 * pair + 16)
                if nth is not None:
                    pe.wait_ge(mask_set, nth[k - 2])
                for r in range(IB):
                    last = nc.tensor.transpose(trb[b][:, r * P:(r + 1) * P],
                                               adj_t[:, half, r, k % OCT * P:(k % OCT + 1) * P], identb[:, :])
                last.then_inc(transposed, 1)

            G_flat = G_words[:, :, :].rearrange("p j c -> p (j c)")
            F_flat = F[:, :, :, :, :].rearrange("p j h s c -> p (j h s c)")
            M_flat = M[:, :, :, :, :].rearrange("p j h s c -> p (j h s c)")

            def chunk(r, h):
                n = r * HEADS + h
                return acc[n // PER_BANK], n % PER_BANK * CH

            def add_block(g_at, f_at, k, nth):
                b = k % NB

                def add(lhsT, flat, start, width, dst):
                    return nc.tensor.matmul(dst, lhsT, flat[:, bass.ds(start, width)], start=False, stop=False,
                                            skip_group_check=True)

                pe.wait_ge(mask_set, nth[k])
                for r in range(IB):
                    h = 0
                    while h < HEADS:
                        bank_h, col = chunk(r, h)
                        n = min(HEADS - h, PER_BANK - col // CH)
                        dst = bank_h[:, col:col + n * CH].rearrange("p (n c) -> p n c", c=CH)[:, :, BC:CH]
                        add(mask[:, k % NM, r * P:(r + 1) * P], M_flat, f_at + (k * HEADS + h) * FC, n * FC, dst)
                        h += n
                for heads, ready, free in (([DVE_HEAD], T_dve, None), ([POOL_HEAD], T_pool, early_done),
                                           (range(POOL_HEAD + 1, ACT_HEADS), T_act, block_done)):
                    pe.wait_ge(ready, nth[k] + LEAD)
                    for h in heads:
                        for flat, at, width, first in ((G_flat, g_at, BC, 0), (F_flat, f_at, FC, BC)):
                            for r in range(IB):
                                bank_h, col = chunk(r, h)
                                last = add(T[:, b, h, r * P:(r + 1) * P], flat, at + (k * HEADS + h) * width, width,
                                           bank_h[:, col + first:col + first + width])
                    if free is not None:
                        last.then_inc(free, 1)

            def octet(g, u, half, ahead=True):
                o, pair = 2 * u + half, g * (OCTS // 2) + u
                nth = counts(pe, g * JB + o * OCT, OCT)
                g_at, f_at = o * (OCT * HEADS * BC), o * (OCT * HEADS * FC)
                if not isinstance(o, int):
                    g_at, f_at = pe.snap(g_at), pe.snap(f_at)
                for k in range(OCT):
                    if k + 2 < OCT or ahead:
                        transpose_block(pair, half, k + 2, nth)
                    add_block(g_at, f_at, k, nth)

            def open_sums(g):
                pe.wait_ge(acc_dve, done(g * (BANKS // 2)))
                pe.wait_ge(acc_act, done(g * (BANKS - BANKS // 2)))
                for b in range(BANKS):
                    nc.tensor.matmul(acc[b][:, USED:USED + 2], identb[:, :], zeros[:, :], start=True, stop=False,
                                     skip_group_check=True)

            def close_sums():
                for b in range(BANKS):
                    last = nc.tensor.matmul(acc[b][:, USED:USED + 2], identb[:, :], zeros[:, :], start=False, stop=True,
                                            skip_group_check=True)
                last.then_inc(acc_done, 1)

            pe.wait_ge(m_set, 1)
            pe.wait_ge(part_set, done(3 * (JB // TJ)))
            pe.wait_ge(s_copied, done(XT))
            for k in range(2):
                transpose_block(0, 0, k)
            with pe.Fori(0, GROUPS - 1) as g:
                open_sums(g)
                with pe.Fori(0, OCTS // 2) as u:
                    for half in range(2):
                        octet(g, u, half)
                close_sums()
            open_sums(GROUPS - 1)
            with pe.Fori(0, OCTS // 2 - 1) as u:
                for half in range(2):
                    octet(GROUPS - 1, u, half)
            for half in range(2):
                octet(GROUPS - 1, OCTS // 2 - 1, half, ahead=half == 0)
            close_sums()


_INS = ["x", "adj", "L0_gnn_W", "L0_gnn_a"]


def kernel(**inputs):
    import numpy as np
    import concourse.bacc as bacc
    from concourse.bass_utils import run_bass_kernel_spmd

    nc = bacc.Bacc("TRN2", target_bir_lowering=False, num_devices=1)
    arrays, args = {}, []
    for name in _INS:
        v = np.ascontiguousarray(inputs[name])
        arrays[f"in_{name}"] = v
        args.append(nc.dram_tensor(f"in_{name}", v.shape, mybir.dt.from_np(v.dtype), kind="ExternalInput").ap())
    shape = inputs["x"].shape
    args.append(nc.dram_tensor("out", shape, mybir.dt.float32, kind="ExternalOutput").ap())
    gat_layernorm(nc, *args)
    r = run_bass_kernel_spmd(nc, [arrays], core_ids=[0])
    return r.results[0]["out"]
```
